# Optimizing a Trainium2 kernel written in Bass

```python
import numpy as np
import jax
import jax.numpy as jnp

def _softmax(x, axis=-1):
    return jax.nn.softmax(x, axis=axis)

def _gelu(x):
    return jax.nn.gelu(x, approximate=True)

def _silu(x):
    return jax.nn.silu(x)

def _sigmoid(x):
    return jax.nn.sigmoid(x)

def _layernorm(x, axis=-1, eps=1e-05):
    m = jnp.mean(x, axis=axis, keepdims=True)
    v = jnp.var(x, axis=axis, keepdims=True)
    return (x - m) / jnp.sqrt(v + eps)

def _scatter_add(tgt, idx, src, axis=0):
    return tgt.at[idx].add(src)

def _segment_sum(src, seg, n):
    return jax.ops.segment_sum(src, seg, n)
kernel_name = 'mk_dlrm_tower_d1_rec_r8_6ca074'

def setup_inputs(seed: int=0):
    np.random.seed(seed)
    _w = jnp.asarray

    def _rec_inputs():
        import jax
        import jax.numpy as jnp
        _tk = jax.random.key(seed)
        dense_ctx = jax.random.normal(jax.random.fold_in(_tk, 190), (1024, 16), jnp.float32)
        ids = jnp.stack([jax.random.randint(jax.random.fold_in(_tk, 200 + f), (1024,), 0, v, jnp.int32) for f, v in enumerate([1250, 125000, 125000, 125000, 1000, 125000, 1000, 125000, 12500, 125000, 12500, 1000, 1250, 12500, 125000, 1250])], axis=1)
        tbl_0 = 0.05 * jax.random.normal(jax.random.fold_in(_tk, 500 + 0), (1250, 16), jnp.float32)
        tbl_1 = 0.05 * jax.random.normal(jax.random.fold_in(_tk, 500 + 1), (125000, 16), jnp.float32)
        tbl_2 = 0.05 * jax.random.normal(jax.random.fold_in(_tk, 500 + 2), (125000, 16), jnp.float32)
        tbl_3 = 0.05 * jax.random.normal(jax.random.fold_in(_tk, 500 + 3), (125000, 16), jnp.float32)
        tbl_4 = 0.05 * jax.random.normal(jax.random.fold_in(_tk, 500 + 4), (1000, 16), jnp.float32)
        tbl_5 = 0.05 * jax.random.normal(jax.random.fold_in(_tk, 500 + 5), (125000, 16), jnp.float32)
        tbl_6 = 0.05 * jax.random.normal(jax.random.fold_in(_tk, 500 + 6), (1000, 16), jnp.float32)
        tbl_7 = 0.05 * jax.random.normal(jax.random.fold_in(_tk, 500 + 7), (125000, 16), jnp.float32)
        tbl_8 = 0.05 * jax.random.normal(jax.random.fold_in(_tk, 500 + 8), (12500, 16), jnp.float32)
        tbl_9 = 0.05 * jax.random.normal(jax.random.fold_in(_tk, 500 + 9), (125000, 16), jnp.float32)
        tbl_10 = 0.05 * jax.random.normal(jax.random.fold_in(_tk, 500 + 10), (12500, 16), jnp.float32)
        tbl_11 = 0.05 * jax.random.normal(jax.random.fold_in(_tk, 500 + 11), (1000, 16), jnp.float32)
        tbl_12 = 0.05 * jax.random.normal(jax.random.fold_in(_tk, 500 + 12), (1250, 16), jnp.float32)
        tbl_13 = 0.05 * jax.random.normal(jax.random.fold_in(_tk, 500 + 13), (12500, 16), jnp.float32)
        tbl_14 = 0.05 * jax.random.normal(jax.random.fold_in(_tk, 500 + 14), (125000, 16), jnp.float32)
        tbl_15 = 0.05 * jax.random.normal(jax.random.fold_in(_tk, 500 + 15), (1250, 16), jnp.float32)
        _rk = jax.random.fold_in(_tk, 7)
        r_x0 = -0.000233584 + 0.999828 * jax.random.normal(jax.random.fold_in(_rk, 101), (1024, 39, 16), jnp.float32)
        W_top1 = 0.0606339 * jax.random.normal(jax.random.fold_in(_tk, 801), (272, 512), jnp.float32)
        W_top2 = 0.0441942 * jax.random.normal(jax.random.fold_in(_tk, 802), (512, 256), jnp.float32)
        W_top3 = 0.0625 * jax.random.normal(jax.random.fold_in(_tk, 803), (256, 1), jnp.float32)
        b_top1 = jnp.zeros((512,), jnp.float32)
        b_top2 = jnp.zeros((256,), jnp.float32)
        return (dense_ctx, ids, tbl_0, tbl_1, tbl_2, tbl_3, tbl_4, tbl_5, tbl_6, tbl_7, tbl_8, tbl_9, tbl_10, tbl_11, tbl_12, tbl_13, tbl_14, tbl_15, r_x0, W_top1, b_top1, W_top2, b_top2, W_top3)
    dense_ctx, ids, tbl_0, tbl_1, tbl_2, tbl_3, tbl_4, tbl_5, tbl_6, tbl_7, tbl_8, tbl_9, tbl_10, tbl_11, tbl_12, tbl_13, tbl_14, tbl_15, r_x0, W_top1, b_top1, W_top2, b_top2, W_top3 = _rec_inputs()

    def _L0_rec_setup():
        import jax, jax.numpy as jnp
        import numpy as np
        B, S, F, D, K = (1024, 16, 39, 16, 16)
        key = jax.random.key(seed)
        k1, k2, k3, k4, k5 = jax.random.split(key, 5)
        xl = jax.random.normal(k1, (B, S, D), dtype=jnp.float32)
        x0 = jax.random.normal(k2, (B, F, D), dtype=jnp.float32)
        w = jnp.broadcast_to(jnp.eye(D, dtype=jnp.float32), (K, D, D)) + 0.02 * jax.random.normal(k3, (K, D, D), dtype=jnp.float32)
        alpha = jnp.ones((S * F, K), dtype=jnp.float32) + 0.02 * jax.random.normal(k4, (S * F, K), dtype=jnp.float32)
        hv = jnp.ones((K, D, 1), dtype=jnp.float32) + 0.02 * jax.random.normal(k5, (K, D, 1), dtype=jnp.float32)
        return {'xl': xl, 'x0': x0, 'w': w, 'alpha': alpha, 'hv': hv}
    _L0_rec_all = _L0_rec_setup()
    _L0_rec_in = {k: v for k, v in _L0_rec_all.items() if k in ('w', 'alpha', 'hv')}
    del _L0_rec_all
    return {'dense_ctx': dense_ctx, 'ids': ids, 'tbl_0': tbl_0, 'tbl_1': tbl_1, 'tbl_2': tbl_2, 'tbl_3': tbl_3, 'tbl_4': tbl_4, 'tbl_5': tbl_5, 'tbl_6': tbl_6, 'tbl_7': tbl_7, 'tbl_8': tbl_8, 'tbl_9': tbl_9, 'tbl_10': tbl_10, 'tbl_11': tbl_11, 'tbl_12': tbl_12, 'tbl_13': tbl_13, 'tbl_14': tbl_14, 'tbl_15': tbl_15, 'r_x0': r_x0, 'W_top1': W_top1, 'b_top1': b_top1, 'W_top2': W_top2, 'b_top2': b_top2, 'W_top3': W_top3, 'L0_rec_w': _L0_rec_in['w'], 'L0_rec_alpha': _L0_rec_in['alpha'], 'L0_rec_hv': _L0_rec_in['hv']}

def reference(dense_ctx, ids, tbl_0, tbl_1, tbl_2, tbl_3, tbl_4, tbl_5, tbl_6, tbl_7, tbl_8, tbl_9, tbl_10, tbl_11, tbl_12, tbl_13, tbl_14, tbl_15, r_x0, W_top1, b_top1, W_top2, b_top2, W_top3, L0_rec_w, L0_rec_alpha, L0_rec_hv):
    import jax
    import jax.numpy as jnp

    def _L0_rec_ref(xl, x0, w, alpha, hv):
        import jax, jax.numpy as jnp
        import numpy as np
        B, S, F, D, K = (1024, 16, 39, 16, 16)
        b, s, d = xl.shape
        f = x0.shape[1]
        A = jnp.repeat(x0, s, axis=1)
        Bm = jnp.repeat(xl, f, axis=2).reshape(b, s * f, d)
        out = jnp.einsum('bnh,bnd,nk,khd,kd->bkh', A, Bm, alpha, w, hv[..., 0])
        return out
    e = jnp.stack([tbl_0[ids[:, 0]], tbl_1[ids[:, 1]], tbl_2[ids[:, 2]], tbl_3[ids[:, 3]], tbl_4[ids[:, 4]], tbl_5[ids[:, 5]], tbl_6[ids[:, 6]], tbl_7[ids[:, 7]], tbl_8[ids[:, 8]], tbl_9[ids[:, 9]], tbl_10[ids[:, 10]], tbl_11[ids[:, 11]], tbl_12[ids[:, 12]], tbl_13[ids[:, 13]], tbl_14[ids[:, 14]], tbl_15[ids[:, 15]]], axis=1)
    z = _L0_rec_ref(e, r_x0, L0_rec_w, L0_rec_alpha, L0_rec_hv)
    z = z.reshape(z.shape[0], -1)
    h = jnp.concatenate([z, dense_ctx], axis=1)
    h = jnp.maximum(h @ W_top1 + b_top1, 0.0)
    h = jnp.maximum(h @ W_top2 + b_top2, 0.0)
    y = h @ W_top3
    return y

_drawn_inputs = setup_inputs


def setup_inputs(seed=0):
    import zlib

    import numpy as np

    out = dict(_drawn_inputs(seed))
    spreads = {'b_top1': (0.0, 0.1), 'b_top2': (0.0, 0.1)}
    factors = {}
    for name, (base, spread) in spreads.items():
        noise = np.random.default_rng([zlib.crc32(name.encode()), seed]).standard_normal(out[name].shape)
        drawn = base * np.exp(spread * noise) if base else spread * noise
        out[name] = jnp.asarray(drawn.astype(out[name].dtype))
    for name, factor in factors.items():
        out[name] = (out[name] * factor).astype(out[name].dtype)
    return out
```

```python
from contextlib import ExitStack

import concourse.bass as bass
from concourse import mybir

F32 = mybir.dt.float32
BF16 = mybir.dt.bfloat16
I32 = mybir.dt.int32
ALU = mybir.AluOpType
ACT = mybir.ActivationFunctionType
AX = mybir.AxisListType

P = 128
B = 1024
T = B // P
S = 16
D = 16
Q = S * D
F = 39
K = 16
H = D
R = 8
GF = P // (2 * R)
G = -(-F // GF)
W = GF * R
HP = H // 2
N1, N2 = 512, 256
M1, M2 = N1 // P, N2 // P
DC = 16
EPAD = 272


def windows():
    width = S * K
    starts = []
    for i in range(F):
        first, last = width * i // F, (width * i + width - 1) // F
        starts.append((max(0, last - R + 1), min(first, Q - R)))
    return starts


def window_runs():
    bounds = windows()
    runs, i = [], 0
    while i < F:
        best = (1, 1, bounds[i][0], 0)
        for q0 in range(bounds[i][0], bounds[i][1] + 1):
            for step in (6, 7):
                n = 0
                while i + n < F:
                    q = q0 + 13 * (n // 2) + step * (n % 2)
                    if not bounds[i + n][0] <= q <= bounds[i + n][1]:
                        break
                    n += 1
                n -= n % 2
                if n > best[0]:
                    best = (n, n // 2, q0, step)
        runs.append((i, best[1], best[2], best[3], best[0]))
        i += best[0]
    return runs


def window_starts():
    starts = []
    for field, pairs, q0, step, n in window_runs():
        starts += [q0 + 13 * (m // 2) + step * (m % 2) for m in range(n)]
    return starts


def tower(nc, ids, tables, x0, w_top1_z, w_top1_d, b_top1, w_top2, b_top2, w_top3, dense_t,
          w_dk, hv_dk, alpha, meets, consts, out):
    runs = window_runs()
    with ExitStack() as ctx:
        def sb(name, shape, dt=F32):
            return ctx.enter_context(nc.sbuf_tensor(name, shape, dt))

        def psum(name, shape, dt=F32):
            return ctx.enter_context(nc.psum_tensor(name, shape, dt))

        def sem(name):
            return ctx.enter_context(nc.semaphore(name))

        ids_sb = sb("ids_sb", [P, T, S], I32)
        cst = sb("cst", [P, P + K + 2])
        ident = cst[:, 0:P]
        same_k = cst[:, P:P + K]
        of_h = cst[:, P + K:P + K + 2]
        meets_sb = sb("meets_sb", [P, G, D, W], BF16)
        alpha_sb = sb("alpha_sb", [P, G, K])
        alpha3 = sb("alpha3", [P, G, 3, K], BF16)
        alpha_r = sb("alpha_r", [P, 2, G, K])
        w_sb = sb("w_sb", [P, 2, H])
        hv_sb = sb("hv_sb", [P, 2])
        wbd = sb("wbd", [P, 2, H, K])
        a1_sb = sb("a1_sb", [W, 2, 2, P])
        a1t_sb = sb("a1t_sb", [P, 2, 2, P])
        coef = sb("coef", [P, G, HP, 2, K])
        w1_sb = sb("w1_sb", [P, 2, N1])
        w1d_sb = sb("w1d_sb", [DC, N1])
        w2_sb = sb("w2_sb", [P, M1, N2])
        w3_sb = sb("w3_sb", [P, M2])
        b1_sb = sb("b1_sb", [P, M1])
        b2_sb = sb("b2_sb", [P, M2])
        dense_sb = sb("dense_sb", [DC, B])
        x0_sb = sb("x0_sb", [P, T, F * H])
        x_rep = sb("x_rep", [P, 2, G, H, GF, R])
        e_sb = sb("e_sb", [P, 2, EPAD])
        e_win = sb("e_win", [P, 2, G * W])
        e_both = sb("e_both", [P, 2, G, 2, W])
        et_sb = sb("et_sb", [P, 2, G, P])
        x_sb = sb("x_sb", [P, 2, HP, P])
        z_sb = sb("z_sb", [P, 2, 2, P])
        h1_sb = sb("h1_sb", [P, M1, P])
        h2_sb = sb("h2_sb", [P, M2, P])
        y_sb = sb("y_sb", [P, T])
        xp = [psum(f"xp{i}", [P, HP, P]) for i in range(2)]
        ep = psum("ep", [P, 4, P])
        hp1 = psum("hp1", [P, M1, P])
        zp = psum("zp", [P, 4, P])
        mp = psum("mp", [P, 4, P])
        e4_ps, y_ps, h2_ps = mp[:, 0, :], mp[:, 1, 0:1], mp[:, 2:4, :]

        s_ids = sem("s_ids")
        s_pad = sem("s_pad")
        rep_pad = sem("rep_pad")
        s_cst = sem("s_cst")
        s_meets = sem("s_meets")
        s_alpha = sem("s_alpha")
        s_w = sem("s_w")
        s_w1 = sem("s_w1")
        s_w2 = sem("s_w2")
        s_x0 = [sem("s_x0_0"), sem("s_x0_1")]
        s_e = [sem("s_e_0"), sem("s_e_1")]
        split_step = sem("split_step")
        alpha_split = sem("alpha_split")
        wbd_ready = sem("wbd_ready")
        a1_done = sem("a1_done")
        a1_copied = sem("a1_copied")
        a1t_done = sem("a1t_done")
        a1t_copied = sem("a1t_copied")
        coef_done = sem("coef_done")
        coef_ready = sem("coef_ready")
        act_step = sem("act_step")
        win_ready = sem("win_ready")
        et_done = sem("et_done")
        et_ready = sem("et_ready")
        rep_ready = sem("rep_ready")
        xt_done = sem("xt_done")
        x_ready = sem("x_ready")
        z_done = sem("z_done")
        z_ready = sem("z_ready")
        h1_done = sem("h1_done")
        h1_ready = sem("h1_ready")
        h2_done = sem("h2_done")
        h2_ready = sem("h2_ready")
        y_done = sem("y_done")
        y_ready = sem("y_ready")
        s_out = sem("s_out")

        def a1_bank(g, dh):
            bank = xp[g % 2][0:W, 4 * dh:4 * dh + 4, :].rearrange("p c b -> p (c b)")
            return bank[:, 0:8 * 3 * K].rearrange("p (d s k) -> p d s k", s=3, k=K)

        block = ctx.enter_context(nc.Block())

        @block.sync
        def _(sp):
            sp.dma_start(ids_sb[:], ids.rearrange("(p t) f -> p t f", t=T)).then_inc(s_ids, 16)
            sp.dma_start(alpha_sb[:], alpha.rearrange("(g n) k -> n g k", n=P)).then_inc(s_alpha, 16)
            sp.dma_start(meets_sb[:], meets).then_inc(s_meets, 16)
            x0_v = x0.rearrange("(p t) i h -> p t (i h)", t=T)
            sp.dma_start(x0_sb[:, 0:2, :], x0_v[:, 0:2, :]).then_inc(s_x0[0], 16)
            sp.dma_start(x0_sb[:, 2:T, :], x0_v[:, 2:T, :]).then_inc(s_x0[1], 16)
            sp.dma_start(w1_sb[:], w_top1_z.rearrange("(q p) n -> p q n", p=P)).then_inc(s_w1, 16)
            sp.dma_start(w1d_sb[:], w_top1_d).then_inc(s_w1, 16)
            sp.dma_start(dense_sb[:], dense_t).then_inc(s_w1, 16)
            sp.dma_start(b1_sb[:], b_top1).then_inc(s_w1, 16)
            sp.dma_start(w2_sb[:], w_top2.rearrange("(m p) n -> p m n", p=P)).then_inc(s_w2, 16)
            sp.dma_start(w3_sb[:], w_top3).then_inc(s_w2, 16)
            sp.dma_start(b2_sb[:], b_top2).then_inc(s_w2, 16)
            sp.wait_ge(y_ready, T)
            sp.dma_start(out.rearrange("(p t) o -> p (t o)", t=T), y_sb[:]).then_inc(s_out, 16)
            sp.wait_ge(s_out, 16)

        @block.gpsimd
        def _(pool):
            nc.gpsimd.memset(e_win[:, :, F * R:], 0.0).then_inc(s_pad, 1)
            nc.gpsimd.memset(x_rep[:, :, G - 1, :, F - (G - 1) * GF:, :], 0.0).then_inc(rep_pad, 1)
            pool.wait_ge(s_ids, 16)

            for t in range(T):
                if t >= 2:
                    pool.wait_ge(win_ready, t - 1)
                for f in range(S):
                    pool.indirect_dma_start(e_sb[:, t % 2, f * D:(f + 1) * D], None, tables[f],
                                            bass.IndirectOffsetOnAxis(ids_sb[:, t, f:f + 1], 0)).then_inc(s_e[t % 2], 16)

        @block.tensor
        def _(pe):
            def a1(g):
                if g >= 2:
                    pe.wait_ge(a1_copied, g - 1)
                for d in range(D):
                    last = nc.tensor.matmul(a1_bank(g, d // 8)[:, d % 8, :, :], meets_sb[:, g, d, :],
                                            alpha3[:, g, :, :], start=True, stop=True)
                last.then_inc(a1_done, 1)

            def a1t_and_coef(g):
                pe.wait_ge(a1_copied, g + 1)
                if g >= 1:
                    pe.wait_ge(a1t_copied, g)
                for dh in range(2):
                    last = nc.tensor.transpose(ep[:, dh, 0:W], a1_sb[:, g % 2, dh, :], ident[0:W, 0:W])
                last.then_inc(a1t_done, 1)
                pe.wait_ge(a1t_copied, g + 1)
                if g >= 1:
                    pe.wait_ge(coef_ready, g)
                for dh in range(2):
                    last = nc.tensor.matmul(hp1[:, 0:2, :].rearrange("p a b -> p (a b)"),
                                            a1t_sb[:, g % 2, dh, :], wbd[:, dh, :, :],
                                            start=(dh == 0), stop=(dh == 1))
                last.then_inc(coef_done, 1)

            pe.wait_ge(s_meets, 16)
            pe.wait_ge(alpha_split, 1)
            a1(0)
            pe.wait_ge(s_cst, 16)
            pe.wait_ge(wbd_ready, 1)
            for g in range(G):
                if g + 1 < G:
                    a1(g + 1)
                a1t_and_coef(g)
            pe.wait_ge(a1_copied, G)
            pe.wait_ge(coef_ready, G)
            pe.wait_ge(s_w1, 64)
            pe.wait_ge(s_w2, 48)

            def x0_turn(t, slot, g):
                pe.wait_ge(rep_ready, t * G + g + 1)
                if not (isinstance(t, int) and t == 0 and g < 2):
                    pe.wait_ge(x_ready, t * G + (g - 1))
                if isinstance(t, int) and t == 0 and g < 2:
                    pe.wait_ge(a1_copied, G)
                for pair in range(HP):
                    last = nc.tensor.transpose(
                        xp[(slot + g) % 2][:, pair, :],
                        x_rep[:, slot, g, 2 * pair:2 * pair + 2, :, :].rearrange("p h i r -> p (h i r)"), ident)
                last.then_inc(xt_done, 1)

            def window_turn(t, slot):
                pe.wait_ge(win_ready, t + 1)
                if not (isinstance(t, int) and t == 0):
                    pe.wait_ge(et_ready, 2 * t)
                if not (isinstance(t, int) and t == 0):
                    pe.wait_ge(z_ready, t)
                for g in range(G):
                    dst = ep[:, g, :] if g < 4 else e4_ps
                    last = nc.tensor.transpose(dst, e_both[:, slot, g, :, :].rearrange("p h w -> p (h w)"), ident)
                last.then_inc(et_done, 1)

            def z_sum(t, slot, g):
                pe.wait_ge(x_ready, t * G + g + 1)
                if g == 0 and not (isinstance(t, int) and t == 0):
                    pe.wait_ge(z_ready, t)
                for pair in range(HP):
                    zh, c = pair // 4, pair % 4
                    last = nc.tensor.matmul(zp[32 * c:32 * c + 32, zh, :],
                                            coef[:, g, pair, :, :].rearrange("p h k -> p (h k)"),
                                            x_sb[:, (slot + g) % 2, pair, :],
                                            start=(g == 0 and zh == 0), stop=(g == G - 1), skip_group_check=True)
                last.then_inc(z_done, 1)

            def layer1(t, slot, ms):
                if 0 in ms:
                    pe.wait_ge(z_ready, t + 1)
                for m in ms:
                    cols = slice(m * P, (m + 1) * P)
                    nc.tensor.matmul(hp1[:, m, :], w1_sb[:, 0, cols], z_sb[:, slot, 0, :], start=True, stop=False)
                    nc.tensor.matmul(hp1[:, m, :], w1_sb[:, 1, cols], z_sb[:, slot, 1, :], start=False, stop=False)
                    last = nc.tensor.matmul(hp1[:, m, :], w1d_sb[:, cols], dense_sb[:, bass.ds(t * P, P)],
                                            start=False, stop=True)
                if M1 - 1 in ms:
                    last.then_inc(h1_done, 1)

            def layer2(t):
                pe.wait_ge(h1_ready, t + 1)
                if isinstance(t, int) and t == T - 1:
                    pe.wait_ge(y_ready, t)
                else:
                    pe.wait_ge(et_ready, 2 * (t + 2))
                for m in range(M2):
                    for k in range(M1):
                        last = nc.tensor.matmul(h2_ps[:, m, :], w2_sb[:, k, m * P:(m + 1) * P], h1_sb[:, k, :],
                                                start=(k == 0), stop=(k == M1 - 1))
                last.then_inc(h2_done, 1)

            def layer3(t):
                pe.wait_ge(h2_ready, t + 1)
                for k in range(M2):
                    last = nc.tensor.matmul(y_ps, h2_sb[:, k, :], w3_sb[:, k:k + 1],
                                            start=(k == 0), stop=(k == M2 - 1))
                last.then_inc(y_done, 1)

            def chunk(t, slot, first=False):
                x0_turn(t, slot, 0)
                x0_turn(t, slot, 1)
                window_turn(t, slot)
                if not first:
                    layer1(t - 1, 1 - slot, [0, 1])
                z_sum(t, slot, 0)
                x0_turn(t, slot, 2)
                if not first:
                    layer1(t - 1, 1 - slot, [2, 3])
                z_sum(t, slot, 1)
                x0_turn(t, slot, 3)
                z_sum(t, slot, 2)
                x0_turn(t, slot, 4)
                if not first:
                    layer2(t - 1)
                z_sum(t, slot, 3)
                z_sum(t, slot, 4)
                if not first:
                    layer3(t - 1)

            chunk(0, 0, first=True)
            with pe.Fori(0, T // 2 - 1) as i:
                chunk(2 * i + 1, 1)
                chunk(2 * i + 2, 0)
            chunk(T - 1, 1)
            layer1(T - 1, 1, [0, 1, 2, 3])
            layer2(T - 1)
            layer3(T - 1)

        @block.vector
        def _(dve):
            steps = [0]

            def step(ins):
                steps[0] += 1
                ins.then_inc(split_step, 1)
                dve.wait_ge(split_step, steps[0])

            dve.wait_ge(s_alpha, 16)
            step(nc.vector.tensor_copy(alpha3[:, :, 0, :], alpha_sb[:]))
            step(nc.vector.tensor_tensor(alpha_r[:, 0], alpha_sb[:], alpha3[:, :, 0, :], ALU.subtract))
            step(nc.vector.tensor_copy(alpha3[:, :, 1, :], alpha_r[:, 0]))
            step(nc.vector.tensor_tensor(alpha_r[:, 1], alpha_r[:, 0], alpha3[:, :, 1, :], ALU.subtract))
            nc.vector.tensor_copy(alpha3[:, :, 2, :], alpha_r[:, 1]).then_inc(alpha_split, 1)
            dve.wait_ge(s_w, 32)
            dve.wait_ge(s_cst, 16)
            for dh in range(2):
                last = nc.vector.scalar_tensor_tensor(
                    out=wbd[:, dh, :, :], in0=w_sb[:, dh, :].unsqueeze(2).broadcast_to([P, H, K]),
                    scalar=hv_sb[:, dh:dh + 1], in1=same_k.unsqueeze(1).broadcast_to([P, H, K]),
                    op0=ALU.mult, op1=ALU.mult)
            last.then_inc(wbd_ready, 1)
            for g in range(G):
                dve.wait_ge(a1_done, g + 1)
                if g >= 2:
                    dve.wait_ge(a1t_done, g - 1)
                for dh in range(2):
                    last = nc.vector.tensor_reduce(
                        a1_sb[:, g % 2, dh, :].rearrange("p (d k) -> p d k", k=K),
                        a1_bank(g, dh).rearrange("p d s k -> p d k s"), AX.X, ALU.add)
                last.then_inc(a1_copied, 1)

            def products(t, slot, g, first=False):
                if g == 0:
                    dve.wait_ge(et_ready, 2 * (t + 1))
                dve.wait_ge(xt_done, t * G + g + 1)
                if not (first and g < 2):
                    dve.wait_ge(z_done, t * G + (g - 1))
                s = (slot + g) % 2
                nc.vector.tensor_tensor(
                    x_sb[:, s, :, :], xp[s][:],
                    et_sb[:, slot, g, :].unsqueeze(1).broadcast_to([P, HP, P]), ALU.mult).then_inc(x_ready, 1)

            for g in range(G):
                products(0, 0, g, first=True)
            with dve.Fori(0, T // 2 - 1) as i:
                for g in range(G):
                    products(2 * i + 1, 1, g)
                for g in range(G):
                    products(2 * i + 2, 0, g)
            for g in range(G):
                products(T - 1, 1, g)

        @block.scalar
        def _(act):
            act.dma_start(cst[:], consts).then_inc(s_cst, 16)
            act.dma_start(w_sb[:], w_dk.rearrange("(q p) h -> p q h", p=P)).then_inc(s_w, 16)
            act.dma_start(hv_sb[:], hv_dk).then_inc(s_w, 16)
            act.wait_ge(s_cst, 16)
            for g in range(G):
                act.wait_ge(a1t_done, g + 1)
                if g >= 2:
                    act.wait_ge(coef_done, g - 1)
                for dh in range(2):
                    last = nc.scalar.copy(a1t_sb[:, g % 2, dh, :].rearrange("p (h w) -> p h w", h=2),
                                          ep[:, dh, 0:W].unsqueeze(1).broadcast_to([P, 2, W]))
                last.then_inc(a1t_copied, 1)
                act.wait_ge(coef_done, g + 1)
                found = hp1[:, 0:2, :].rearrange("p a b -> p (a b)").rearrange("p (c h k) -> p c h k", h=2, k=K)
                for h in range(2):
                    last = nc.scalar.activation(coef[:, g, :, h, :], found[:, :, h, :], ACT.Copy,
                                                scale=of_h[:, h:h + 1])
                last.then_inc(coef_ready, 1)

            def repeat_x0(t, slot, gs):
                for g in gs:
                    if g == 0 and isinstance(t, int) and t < 3:
                        act.wait_ge(s_x0[min(t, 2) // 2], 16)
                    if g == 0 and not (isinstance(t, int) and t < 2):
                        act.wait_ge(xt_done, (t - 1) * G)
                    n = min(GF, F - g * GF)
                    src = x0_sb[:, bass.ds(t, 1), g * GF * H:(g * GF + n) * H]
                    nc.scalar.copy(x_rep[:, slot, g, :, 0:n, :],
                                   src.rearrange("p t (i h) -> p (t h) i", h=H).unsqueeze(3)
                                   .broadcast_to([P, H, n, R])).then_inc(rep_ready, 1)

            def take_windows(t, slot, uses):
                act.wait_ge(s_e[slot], 16 * S * (uses + 1))
                if not (isinstance(t, int) and t < 2):
                    act.wait_ge(et_done, t - 1)
                for field, pairs, q0, stp, n in runs:
                    base = e_sb[:, slot, q0:q0 + R]
                    dst = e_win[:, slot, field * R:(field + n) * R]
                    if n == 1:
                        last = nc.scalar.copy(dst, base)
                    else:
                        src = bass.AP(tensor=base.tensor, offset=base.offset,
                                      ap=[base.ap[0], [13, pairs], [stp, 2], [1, R]])
                        last = nc.scalar.copy(dst.rearrange("p (j m r) -> p j m r", m=2, r=R), src)
                last.then_inc(act_step, 1)
                act.wait_ge(act_step, t + 1)
                nc.scalar.copy(e_both[:, slot], e_win[:, slot, :].rearrange("p (g w) -> p g w", w=W)
                               .unsqueeze(2).broadcast_to([P, G, 2, W])).then_inc(win_ready, 1)

            def copy_windows(t, slot):
                act.wait_ge(et_done, t + 1)
                nc.scalar.copy(et_sb[:, slot, 0:4, :], ep[:]).then_inc(et_ready, 1)
                nc.scalar.copy(et_sb[:, slot, G - 1, :], mp[:, 0, :]).then_inc(et_ready, 1)

            def copy_z(t, slot):
                act.wait_ge(z_done, (t + 1) * G)
                nc.scalar.copy(z_sb[:, slot, :, :], zp[:, 0:2, :]).then_inc(z_ready, 1)

            def relu1(t):
                act.wait_ge(h1_done, t + 1)
                for m in range(M1):
                    last = nc.scalar.activation(h1_sb[:, m, :], hp1[:, m, :], ACT.Relu, bias=b1_sb[:, m:m + 1])
                last.then_inc(h1_ready, 1)

            def relu2(t):
                act.wait_ge(h2_done, t + 1)
                for m in range(M2):
                    last = nc.scalar.activation(h2_sb[:, m, :], h2_ps[:, m, :], ACT.Relu, bias=b2_sb[:, m:m + 1])
                last.then_inc(h2_ready, 1)

            def copy_y(t):
                act.wait_ge(y_done, t + 1)
                nc.scalar.copy(y_sb[:, bass.ds(t, 1)], y_ps).then_inc(y_ready, 1)

            def chunk(t, slot, uses, first=False, last=False):
                copy_windows(t, slot)
                if not last:
                    repeat_x0(t + 1, 1 - slot, [0, 1])
                if not first:
                    relu1(t - 1)
                if not last:
                    repeat_x0(t + 1, 1 - slot, [2, 3, 4])
                if not first:
                    relu2(t - 1)
                if not last:
                    take_windows(t + 1, 1 - slot, uses + slot)
                if not first:
                    copy_y(t - 1)
                copy_z(t, slot)

            act.wait_ge(s_w1, 64)
            act.wait_ge(s_w2, 48)
            act.wait_ge(s_pad, 1)
            act.wait_ge(rep_pad, 1)
            repeat_x0(0, 0, range(G))
            take_windows(0, 0, 0)
            chunk(0, 0, 0, first=True)
            with act.Fori(0, T // 2 - 1) as i:
                chunk(2 * i + 1, 1, i)
                chunk(2 * i + 2, 0, i + 1)
            chunk(T - 1, 1, T // 2 - 1, last=True)
            relu1(T - 1)
            relu2(T - 1)
            copy_y(T - 1)


def kernel(**inputs):
    import numpy as np
    import ml_dtypes
    import concourse.bacc as bacc
    from concourse.bass_utils import run_bass_kernel_spmd as run

    nc = bacc.Bacc("TRN2", target_bir_lowering=False, num_devices=1)
    arrays = {}

    def give(name, a):
        a = np.ascontiguousarray(a)
        arrays["in_" + name] = a
        return nc.dram_tensor("in_" + name, a.shape, mybir.dt.from_np(a.dtype), kind="ExternalInput").ap()

    dense = np.asarray(inputs["dense_ctx"])
    w_top1 = np.asarray(inputs["W_top1"])
    ids = give("ids", inputs["ids"])
    tables = [give(f"tbl_{f}", inputs[f"tbl_{f}"]) for f in range(S)]
    x0 = give("r_x0", inputs["r_x0"])
    w_top1_z = give("w_top1_z", w_top1[0:K * H].reshape(K, H, N1).transpose(1, 0, 2).reshape(K * H, N1))
    w_top1_d = give("w_top1_d", w_top1[K * H:])
    b_top1 = give("b_top1", np.asarray(inputs["b_top1"]).reshape(M1, P).T)
    w_top2 = give("w_top2", inputs["W_top2"])
    b_top2 = give("b_top2", np.asarray(inputs["b_top2"]).reshape(M2, P).T)
    w_top3 = give("w_top3", np.asarray(inputs["W_top3"]).reshape(M2, P).T)
    dense_t = give("dense_t", dense.reshape(P, T, DC).transpose(2, 1, 0).reshape(DC, B))
    w_dk = give("w_dk", np.asarray(inputs["L0_rec_w"]).transpose(2, 0, 1).reshape(D * K, H))
    hv_dk = give("hv_dk", np.asarray(inputs["L0_rec_hv"])[:, :, 0].T.reshape(2, P).T)
    alpha_rows = np.zeros((G * P, K), np.float32)
    alpha_rows[0:S * F] = np.asarray(inputs["L0_rec_alpha"])
    alpha = give("alpha", alpha_rows)

    starts = np.array(window_starts())
    n = np.arange(P)[:, None, None, None, None]
    g = np.arange(G)[None, :, None, None, None]
    d = np.arange(D)[None, None, :, None, None]
    i = np.arange(GF)[None, None, None, :, None]
    r = np.arange(R)[None, None, None, None, :]
    field = g * GF + i
    flat = D * (g * P + n) + d
    meet = (n // S == i) & (field < F) & (flat // F == starts[np.minimum(field, F - 1)] + r)
    meets = give("meets", meet.reshape(P, G, D, W).astype(ml_dtypes.bfloat16))
    p = np.arange(P)[:, None]
    of_h = p // W == np.arange(2)[None, :]
    consts = give("consts", np.concatenate(
        [np.eye(P), p % K == np.arange(K)[None, :], of_h], axis=1).astype(np.float32))
    out = nc.dram_tensor("out_y", (B, 1), F32, kind="ExternalOutput").ap()

    tower(nc, ids, tables, x0, w_top1_z, w_top1_d, b_top1, w_top2, b_top2, w_top3, dense_t,
          w_dk, hv_dk, alpha, meets, consts, out)
    result = run(nc, [arrays], core_ids=[0])
    return result.results[0]["out_y"]
```

```python
from contextlib import ExitStack

import concourse.bass as bass
from concourse import mybir

F32 = mybir.dt.float32
BF16 = mybir.dt.bfloat16
F16 = mybir.dt.float16
I32 = mybir.dt.int32
ALU = mybir.AluOpType
ACT = mybir.ActivationFunctionType
AX = mybir.AxisListType

P = 128
B = 1024
T = B // P
S = 16
D = 16
Q = S * D
F = 39
K = 16
H = D
R = 8
GF = P // (2 * R)
G = -(-F // GF)
W = GF * R
HI = 2 * GF
HP = H // 2
N1, N2 = 512, 256
M1, M2 = N1 // P, N2 // P
DC = 16
EPAD = Q + 2 * R
GA = 3
FIELDS_A = 10
LP = 125
LMAX = 10
T2 = T // 2
HB = T2 * P


def window_grid():
    width = S * K
    grid = []
    for g in range(G):
        fields = range(g * GF, min((g + 1) * GF, F))
        bounds = [(max(0, (width * i + width - 1) // F - R + 1), width * i // F) for i in fields]
        fits = [(q0, step) for q0 in range(bounds[0][0], bounds[0][1] + 1) for step in (6, 7)
                if all(lo <= q0 + 13 * (n // 2) + step * (n % 2) <= hi for n, (lo, hi) in enumerate(bounds))]
        grid.append(fits[0])
    return grid


GRID = window_grid()
assert GRID[GA][0] >= FIELDS_A * D - R and GRID[GA - 1][0] + 13 * 3 + 7 + R <= FIELDS_A * D


def small_tables(rows):
    return [(f, n // LP) for f, n in enumerate(rows) if n % LP == 0 and n <= LP * LMAX]


def tower(nc, ids, small_ids, tables, tab_small, x0, w_top1_z, w_top1_d, w_top2, dense_t, params, meets, consts,
          small, out):
    NS = len(small)
    AT = [sum(j for f, j in small[:n]) for n in range(NS + 1)]
    SLOTS = AT[NS]
    large = [f for f in range(S) if f not in [f for f, j in small]]
    large_a = [f for f in large if f < FIELDS_A]
    large_b = [f for f in large if f >= FIELDS_A]
    late = [[n for n in (2 * t, 2 * t + 1) if n < NS] for t in range(3)]
    assert sum(len(n) for n in late) == NS

    with ExitStack() as ctx:
        def sb(name, shape, dt=F32):
            return ctx.enter_context(nc.sbuf_tensor(name, shape, dt))

        def psum(name, shape, dt=F32):
            return ctx.enter_context(nc.psum_tensor(name, shape, dt))

        def sem(name):
            return ctx.enter_context(nc.semaphore(name))

        ids_sb = sb("ids_sb", [P, T, S], I32)
        cst = sb("cst", [P, P + K + 2 + SLOTS])
        ident = cst[:, 0:P]
        same_k = cst[:, P:P + K]
        of_h = cst[:, P + K:P + K + 2]
        slot_row = cst[:, P + K + 2:]
        meets_sb = sb("meets_sb", [P, G, D, W], BF16)
        params_sb = sb("params_sb", [P, G * K + 2 * H + 2 + M1 + 2 * M2])
        alpha_sb = params_sb[:, 0:G * K].rearrange("p (g k) -> p g k", k=K)
        w_sb = params_sb[:, G * K:G * K + 2 * H].rearrange("p (q h) -> p q h", h=H)
        hv_sb = params_sb[:, G * K + 2 * H:G * K + 2 * H + 2]
        b1_sb = params_sb[:, G * K + 2 * H + 2:][:, 0:M1]
        b2_sb = params_sb[:, G * K + 2 * H + 2 + M1:][:, 0:M2]
        w3_sb = params_sb[:, G * K + 2 * H + 2 + M1 + M2:]
        alpha_pad = sb("alpha_pad", [P, G, 3, 2 * P - K], BF16)
        alpha3 = alpha_pad[:, :, :, P - K:P]
        alpha_r = sb("alpha_r", [P, 2, G, K])
        wbd = sb("wbd", [P, 2, H, K])
        a1t_sb = sb("a1t_sb", [P, 2, 2, P])
        coef = sb("coef", [P, G, HP, 2, K])
        w1_sb = sb("w1_sb", [P, 2, N1])
        w1d_sb = sb("w1d_sb", [DC, N1])
        w2_sb = sb("w2_sb", [P, M1, N2])
        dense_sb = sb("dense_sb", [DC, B])
        tab_sb = sb("tab_sb", [LP, SLOTS, D])
        tab3 = sb("tab3", [LP, SLOTS, 3, D], BF16)
        tab_r = sb("tab_r", [LP, SLOTS, D])
        ids_bc = sb("ids_bc", [LP, NS, B], F16)
        onehot = sb("onehot", [LP, SLOTS, HB], BF16)
        x_rep = sb("x_rep", [P, 2, G, HP, P])
        e_sb = sb("e_sb", [P, T, EPAD])
        e_both = sb("e_both", [P, 2, G, R, 2, GF])
        early = sb("early", [P, max(G * HP * P, NS * B)])
        x_sb = early[:, 0:G * HP * P].rearrange("p (g c b) -> p g c b", g=G, c=HP)
        ids_wide = early[0:LP, 0:NS * B].bitcast(I32).rearrange("p (a n b) -> p a n b", a=2, n=NS)
        z_sb = sb("z_sb", [P, 2, 2, P])
        h1_sb = sb("h1_sb", [P, M1, P])
        h2_sb = sb("h2_sb", [P, M2, P])
        y_sb = sb("y_sb", [P, T])
        ea = [psum(f"ea{i}", [P, 4, P]) for i in range(2)]
        eb = [psum(f"eb{i}", [P, 4, P]) for i in range(2)]
        hp1 = [psum(f"hp1_{i}", [P, 4, P]) for i in range(2)]
        zp = psum("zp", [P, 4, P])
        hp2 = psum("hp2", [P, 4, P])
        h2_ps, y_ps = hp2[:, 0:M2, :], hp2[:, M2, 0:1]

        s_ids = sem("s_ids")
        s_cst = sem("s_cst")
        s_params = sem("s_params")
        s_meets = [sem(f"s_meets_{i}") for i in range(3)]
        s_small_ids = [sem(f"s_small_ids_{i}") for i in range(4)]
        s_tab = sem("s_tab")
        s_w1 = sem("s_w1")
        s_w2 = sem("s_w2")
        s_xa = [sem("s_xa_0"), sem("s_xa_1")]
        s_xb = [sem("s_xb_0"), sem("s_xb_1")]
        s_ea = [sem("s_ea_0"), sem("s_ea_1")]
        s_eb = [sem("s_eb_0"), sem("s_eb_1")]
        e_pad = sem("e_pad")
        ids_cast = sem("ids_cast")
        tab_step = sem("tab_step")
        tab_ready = sem("tab_ready")
        oh_ready = sem("oh_ready")
        oh_done = sem("oh_done")
        oh_taken = sem("oh_taken")
        split_step = sem("split_step")
        alpha_split = sem("alpha_split")
        wbd_ready = sem("wbd_ready")
        pad_ready = sem("pad_ready")
        a1t_done = sem("a1t_done")
        a1t_copied = sem("a1t_copied")
        coef_done = sem("coef_done")
        coef_ready = sem("coef_ready")
        wina_ready = sem("wina_ready")
        winb_ready = sem("winb_ready")
        eta_done = sem("eta_done")
        etb_done = sem("etb_done")
        x_ready = sem("x_ready")
        z_done = sem("z_done")
        z_ready = sem("z_ready")
        h1_done = sem("h1_done")
        h1_ready = sem("h1_ready")
        h2_done = sem("h2_done")
        h2_ready = sem("h2_ready")
        y_done = sem("y_done")
        y_ready = sem("y_ready")
        s_out = sem("s_out")

        def flat(bank):
            return bank.rearrange("p a b -> p (a b)")

        def a1t_bank(g):
            return [zp, hp2][g % 2][:, 0:2, 0:W]

        def coef_bank(g):
            return flat(ea[g % 2][:, 0:2, :])

        def oh_bank(half, n):
            bank = [eb, hp1][half][n % 2]
            return flat(bank[:])[:, 0:T2 * 3 * D].rearrange("p (t s d) -> p t s d", s=3, d=D)

        block = ctx.enter_context(nc.Block())

        @block.sync
        def _(sp):
            sp.dma_start(ids_sb[:], ids.rearrange("(p t) f -> p t f", t=T)).then_inc(s_ids, 16)
            def load_small_ids(half, ns, landed):
                sp.dma_start(ids_wide[:, half, ns, :],
                             small_ids[:, half, ns, :].broadcast_to([LP, ns.stop - ns.start, HB])).then_inc(landed, 16)

            def load_meets(n, gs):
                sp.dma_start(meets_sb[:, gs], meets[:, gs]).then_inc(s_meets[n], 16)

            load_small_ids(0, slice(0, 1), s_small_ids[0])
            sp.dma_start(params_sb[:], params).then_inc(s_params, 16)
            sp.dma_start(cst[:], consts).then_inc(s_cst, 16)
            load_meets(0, slice(0, 1))
            sp.dma_start(tab_sb[:], tab_small).then_inc(s_tab, 16)
            load_small_ids(0, slice(1, 3), s_small_ids[1])
            load_meets(1, slice(1, 3))
            load_small_ids(0, slice(3, NS), s_small_ids[2])
            load_meets(2, slice(3, G))
            load_small_ids(1, slice(0, NS), s_small_ids[3])

            def load_x0(t, slot, gs, landed):
                src = x0[bass.ds(t, 1), gs.start:gs.stop].rearrange("t g q n -> q (t g) n")
                for place in range(R):
                    sp.dma_start(x_rep[HI * place:HI * (place + 1), slot, gs.start:gs.stop, :, :]
                                 .rearrange("q g c b -> q g (c b)"), src).then_inc(landed, 16)

            load_x0(0, 0, range(GA), s_xa[0])
            load_x0(0, 0, range(GA, G), s_xb[0])
            sp.dma_start(w1_sb[:], w_top1_z.rearrange("(q p) n -> p q n", p=P)).then_inc(s_w1, 16)
            sp.dma_start(w1d_sb[:], w_top1_d).then_inc(s_w1, 16)
            sp.dma_start(dense_sb[:], dense_t).then_inc(s_w1, 16)
            sp.dma_start(w2_sb[:], w_top2.rearrange("(m p) n -> p m n", p=P)).then_inc(s_w2, 16)
            load_x0(1, 1, range(GA), s_xa[1])
            load_x0(1, 1, range(GA, G), s_xb[1])
            with sp.Fori(1, T // 2) as i:
                for slot in range(2):
                    sp.wait_ge(x_ready, (2 * i + slot - 2) * G + GA)
                    load_x0(2 * i + slot, slot, range(GA), s_xa[slot])
                    sp.wait_ge(x_ready, (2 * i + slot - 1) * G)
                    load_x0(2 * i + slot, slot, range(GA, G), s_xb[slot])
            sp.wait_ge(y_ready, T)
            sp.dma_start(out.rearrange("(p t) o -> p (t o)", t=T), y_sb[:]).then_inc(s_out, 16)
            sp.wait_ge(s_out, 16)

        @block.gpsimd
        def _(pool):
            nc.gpsimd.memset(e_sb[:, :, Q:], 0.0).then_inc(e_pad, 1)
            pool.wait_ge(s_ids, 16)
            for t in range(T):
                for s_e, fields in ((s_ea, large_a), (s_eb, large_b)):
                    if t >= 2:
                        pool.wait_ge(s_e[t % 2], 16 * len(fields) * (t // 2))
                    for f in fields:
                        pool.indirect_dma_start(e_sb[:, t, f * D:(f + 1) * D], None, tables[f],
                                                bass.IndirectOffsetOnAxis(ids_sb[:, t, f:f + 1], 0))\
                            .then_inc(s_e[t % 2], 16)

        @block.tensor
        def _(pe):
            def look_up(half, n):
                pe.wait_ge(oh_ready, half * NS + n + 1)
                if half == 0 and n >= 2:
                    pe.wait_ge(oh_taken, n - 1)
                for c in range(T2):
                    for j in range(AT[n], AT[n + 1]):
                        last = nc.tensor.matmul(oh_bank(half, n)[:, c, :, :], onehot[:, j, c * P:(c + 1) * P],
                                                tab3[:, j, :, :], start=(j == AT[n]), stop=(j == AT[n + 1] - 1))
                last.then_inc(oh_done, 1)

            def a1t(g):
                if g in (0, 1, 3):
                    pe.wait_ge(s_meets[(g + 1) // 2], 16)
                if g >= 2:
                    pe.wait_ge(a1t_copied, g - 1)
                for dh in range(2):
                    for d in range(D // 2):
                        for part in range(3):
                            first = dh == 0 and d == 0 and part == 0
                            last = nc.tensor.matmul(
                                a1t_bank(g)[:, dh, :], alpha_pad[:, g, part, P - K - K * d:2 * P - K - K * d],
                                meets_sb[:, g, dh * D // 2 + d, :], start=first,
                                stop=(d == D // 2 - 1 and part == 2), skip_group_check=True)
                last.then_inc(a1t_done, 1)

            def coefficients(g):
                pe.wait_ge(a1t_copied, g + 1)
                if g >= 2:
                    pe.wait_ge(coef_ready, g - 1)
                for dh in range(2):
                    last = nc.tensor.matmul(coef_bank(g), a1t_sb[:, g % 2, dh, :], wbd[:, dh, :, :],
                                            start=(dh == 0), stop=(dh == 1))
                last.then_inc(coef_done, 1)

            pe.wait_ge(alpha_split, 1)
            a1t(0)
            a1t(1)
            pe.wait_ge(wbd_ready, 1)
            pe.wait_ge(s_cst, 16)
            coefficients(0)
            a1t(2)
            coefficients(1)
            pe.wait_ge(tab_ready, 1)
            for n in range(NS):
                look_up(0, n)
                if n + 3 < G:
                    a1t(n + 3)
                if n + 2 < G:
                    coefficients(n + 2)
            pe.wait_ge(oh_taken, NS)

            def windows_a(t, slot):
                pe.wait_ge(wina_ready, t + 1)
                for g in range(GA):
                    last = nc.tensor.transpose(ea[slot][:, g, :],
                                               e_both[:, slot, g].rearrange("p r h i -> p (r h i)"), ident)
                last.then_inc(eta_done, 1)

            def windows_b(t, slot):
                pe.wait_ge(winb_ready, t + 1)
                for g in range(GA, G):
                    last = nc.tensor.transpose(eb[slot][:, g - GA, :],
                                               e_both[:, slot, g].rearrange("p r h i -> p (r h i)"), ident)
                last.then_inc(etb_done, 1)

            def z_sum(t, slot, g):
                pe.wait_ge(x_ready, t * G + g + 1)
                for pair in range(HP):
                    zh, c = pair // 4, pair % 4
                    last = nc.tensor.matmul(zp[32 * c:32 * c + 32, zh, :],
                                            coef[:, g, pair, :, :].rearrange("p h k -> p (h k)"),
                                            x_sb[:, g, pair, :],
                                            start=(g == 0 and zh == 0), stop=(g == G - 1), skip_group_check=True)
                last.then_inc(z_done, 1)

            def layer1(t, slot):
                for m in range(M1):
                    nc.tensor.matmul(hp1[m // 2][:, m % 2, :], w1d_sb[:, m * P:(m + 1) * P],
                                     dense_sb[:, bass.ds(t * P, P)], start=(m % 2 == 0), stop=False,
                                     skip_group_check=True)
                pe.wait_ge(z_ready, t + 1)
                for half in range(2):
                    for m in range(M1 // 2):
                        cols = slice((2 * half + m) * P, (2 * half + m + 1) * P)
                        for k in range(2):
                            last = nc.tensor.matmul(hp1[half][:, m, :], w1_sb[:, k, cols], z_sb[:, slot, k, :],
                                                    start=False, stop=(k == 1), skip_group_check=True)
                    last.then_inc(h1_done, 1)

            def layer2(t):
                for k in range(M1):
                    pe.wait_ge(h1_ready, M1 * t + k + 1)
                    for m in range(M2):
                        last = nc.tensor.matmul(h2_ps[:, m, :], w2_sb[:, k, m * P:(m + 1) * P], h1_sb[:, k, :],
                                                start=(k == 0 and m == 0), stop=(k == M1 - 1), skip_group_check=True)
                last.then_inc(h2_done, 1)

            def layer3(t):
                pe.wait_ge(h2_ready, t + 1)
                for k in range(M2):
                    last = nc.tensor.matmul(y_ps, h2_sb[:, k, :], w3_sb[:, k:k + 1],
                                            start=(k == 0), stop=(k == M2 - 1))
                last.then_inc(y_done, 1)

            def chunk(t, slot, first=False, last=False, looked_up=0):
                if not first:
                    if looked_up:
                        pe.wait_ge(oh_taken, looked_up)
                    layer1(t - 1, 1 - slot)
                windows_b(t, slot)
                z_sum(t, slot, 0)
                z_sum(t, slot, 1)
                if not first:
                    layer2(t - 1)
                lookups = late[t] if isinstance(t, int) and t < len(late) else []
                for n in lookups[0:1]:
                    look_up(1, n)
                z_sum(t, slot, 2)
                if not last:
                    windows_a(t + 1, 1 - slot)
                z_sum(t, slot, 3)
                for n in lookups[1:]:
                    look_up(1, n)
                if not first:
                    layer3(t - 1)
                z_sum(t, slot, 4)

            pe.wait_ge(coef_ready, G)
            windows_a(0, 0)
            pe.wait_ge(s_w1, 48)
            pe.wait_ge(s_w2, 16)
            chunk(0, 0, first=True)
            chunk(1, 1, looked_up=NS + late[0][-1] + 1)
            chunk(2, 0, looked_up=NS + late[1][-1] + 1)
            pe.wait_ge(oh_taken, 2 * NS)
            with pe.Fori(0, 2) as i:
                chunk(2 * i + 3, 1)
                chunk(2 * i + 4, 0)
            chunk(T - 1, 1, last=True)
            layer1(T - 1, 1)
            layer2(T - 1)
            layer3(T - 1)

        @block.vector
        def _(dve):
            steps = [0]

            def step(ins):
                steps[0] += 1
                ins.then_inc(split_step, 1)
                dve.wait_ge(split_step, steps[0])

            def make_onehots(half, n):
                dve.wait_ge(ids_cast, half * NS + n + 1)
                if half == 1:
                    dve.wait_ge(oh_done, n + 1)
                for j in range(AT[n], AT[n + 1]):
                    last = nc.vector.tensor_scalar(onehot[:, j, :], ids_bc[:, n, half * HB:(half + 1) * HB],
                                                   slot_row[0:LP, j:j + 1], None, ALU.is_equal)
                last.then_inc(oh_ready, 1)

            def take_rows(half, n):
                dve.wait_ge(oh_done, half * NS + n + 1)
                f = small[n][0]
                nc.vector.tensor_reduce(e_sb[:, T2 * half:T2 * (half + 1), f * D:(f + 1) * D],
                                        oh_bank(half, n).rearrange("p t s d -> p t d s"),
                                        AX.X, ALU.add).then_inc(oh_taken, 1)

            nc.vector.memset(alpha_pad[:], 0.0).then_inc(pad_ready, 1)
            dve.wait_ge(pad_ready, 1)
            dve.wait_ge(s_params, 16)
            step(nc.vector.tensor_copy(alpha3[:, :, 0, :], alpha_sb))
            step(nc.vector.tensor_tensor(alpha_r[:, 0], alpha_sb, alpha3[:, :, 0, :], ALU.subtract))
            step(nc.vector.tensor_copy(alpha3[:, :, 1, :], alpha_r[:, 0]))
            nc.vector.tensor_tensor(alpha3[:, :, 2, :], alpha_r[:, 0], alpha3[:, :, 1, :], ALU.subtract)\
              .then_inc(alpha_split, 1)
            dve.wait_ge(s_cst, 16)
            for dh in range(2):
                last = nc.vector.scalar_tensor_tensor(
                    out=wbd[:, dh, :, :], in0=w_sb[:, dh, :].unsqueeze(2).broadcast_to([P, H, K]),
                    scalar=hv_sb[:, dh:dh + 1], in1=same_k.unsqueeze(1).broadcast_to([P, H, K]),
                    op0=ALU.mult, op1=ALU.mult)
            last.then_inc(wbd_ready, 1)
            for n in range(NS):
                make_onehots(0, n)
                if n == 1:
                    dve.wait_ge(tab_step, 1)
                    nc.vector.tensor_tensor(tab_r[:], tab_sb[:], tab3[:, :, 0, :], ALU.subtract).then_inc(tab_step, 1)
                if n == 2:
                    dve.wait_ge(tab_step, 3)
                    nc.vector.tensor_tensor(tab3[:, :, 2, :], tab_r[:], tab3[:, :, 1, :], ALU.subtract)\
                      .then_inc(tab_ready, 1)
                if n >= 2:
                    take_rows(0, n - 2)
            take_rows(0, NS - 2)
            take_rows(0, NS - 1)

            def products(t, slot, uses, g):
                if isinstance(t, int) and t == 0 and g == 0:
                    dve.wait_ge(ids_cast, 2 * NS)
                if g == 0:
                    dve.wait_ge(s_xa[slot], 16 * R * (uses + 1))
                    dve.wait_ge(eta_done, t + 1)
                if g == GA:
                    dve.wait_ge(s_xb[slot], 16 * R * (uses + 1))
                    dve.wait_ge(etb_done, t + 1)
                if not (isinstance(t, int) and t == 0):
                    dve.wait_ge(z_done, (t - 1) * G + g + 1)
                window = ea[slot][:, g, :] if g < GA else eb[slot][:, g - GA, :]
                nc.vector.tensor_tensor(x_sb[:, g, :, :], x_rep[:, slot, g, :, :],
                                        window.unsqueeze(1).broadcast_to([P, HP, P]), ALU.mult).then_inc(x_ready, 1)

            for t in range(3):
                for g in range(G):
                    products(t, t % 2, t // 2, g)
                    if g % 2 == 0 and g // 2 < len(late[t]):
                        make_onehots(1, late[t][g // 2])
                    if g == GA:
                        take_rows(1, late[t][0])
                for n in late[t][1:]:
                    take_rows(1, n)
            with dve.Fori(0, 2) as i:
                for g in range(G):
                    products(2 * i + 3, 1, i + 1, g)
                for g in range(G):
                    products(2 * i + 4, 0, i + 2, g)
            for g in range(G):
                products(T - 1, 1, T // 2 - 1, g)

        @block.scalar
        def _(act):
            def cast_ids(half, n):
                nc.scalar.copy(ids_bc[:, n, half * HB:(half + 1) * HB], ids_wide[:, half, n, :]).then_inc(ids_cast, 1)

            def copy_a1t(g):
                act.wait_ge(a1t_done, g + 1)
                if g >= 2:
                    act.wait_ge(coef_done, g - 1)
                for dh in range(2):
                    last = nc.scalar.copy(
                        a1t_sb[:, g % 2, dh, :].rearrange("p (r h i) -> p r h i", h=2, i=GF),
                        a1t_bank(g)[:, dh, :].rearrange("p (r i) -> p r i", i=GF).unsqueeze(2).broadcast_to([P, R, 2, GF]))
                last.then_inc(a1t_copied, 1)

            def copy_coefficients(g):
                act.wait_ge(coef_done, g + 1)
                found = coef_bank(g).rearrange("p (c h k) -> p c h k", h=2, k=K)
                for h in range(2):
                    last = nc.scalar.activation(coef[:, g, :, h, :], found[:, :, h, :], ACT.Copy,
                                                scale=of_h[:, h:h + 1])
                last.then_inc(coef_ready, 1)

            def take_windows(t, slot, gs):
                for g in gs:
                    q0, stp = GRID[g]
                    base = e_sb[:, bass.ds(t, 1), q0:q0 + R]
                    src = bass.AP(tensor=base.tensor, offset=base.offset,
                                  ap=[base.ap[0], [1, R], [0, 2], [13, GF // 2], [stp, 2]])
                    last = nc.scalar.copy(e_both[:, slot, g].rearrange("p r h (j m) -> p r h j m", m=2), src)
                return last

            def windows_a(t, slot, uses):
                act.wait_ge(s_ea[slot], 16 * len(large_a) * (uses + 1))
                if not (isinstance(t, int) and t < 2):
                    act.wait_ge(eta_done, t - 1)
                take_windows(t, slot, range(GA)).then_inc(wina_ready, 1)

            def windows_b(t, slot, uses):
                act.wait_ge(s_eb[slot], 16 * len(large_b) * (uses + 1))
                if not (isinstance(t, int) and t < 2):
                    act.wait_ge(etb_done, t - 1)
                take_windows(t, slot, range(GA, G)).then_inc(winb_ready, 1)

            def copy_z(t, slot):
                act.wait_ge(z_done, (t + 1) * G)
                nc.scalar.copy(z_sb[:, slot, :, :], zp[:, 0:2, :]).then_inc(z_ready, 1)

            def relu1(t):
                for m in range(M1):
                    act.wait_ge(h1_done, 2 * t + 1 + m // 2)
                    nc.scalar.activation(h1_sb[:, m, :], hp1[m // 2][:, m % 2, :], ACT.Relu,
                                         bias=b1_sb[:, m:m + 1]).then_inc(h1_ready, 1)

            def relu2(t):
                act.wait_ge(h2_done, t + 1)
                for m in range(M2):
                    last = nc.scalar.activation(h2_sb[:, m, :], h2_ps[:, m, :], ACT.Relu, bias=b2_sb[:, m:m + 1])
                last.then_inc(h2_ready, 1)

            def copy_y(t):
                act.wait_ge(y_done, t + 1)
                nc.scalar.copy(y_sb[:, bass.ds(t, 1)], y_ps).then_inc(y_ready, 1)

            def chunk(t, slot, uses, first=False, last=False, late_rows=False):
                windows_b(t, slot, uses)
                if not first:
                    relu1(t - 1)
                if late_rows:
                    act.wait_ge(oh_taken, 2 * NS)
                if not last:
                    windows_a(t + 1, 1 - slot, uses + slot)
                if not first:
                    relu2(t - 1)
                    copy_y(t - 1)
                copy_z(t, slot)

            act.wait_ge(s_small_ids[0], 16)
            cast_ids(0, 0)
            act.wait_ge(s_tab, 16)
            nc.scalar.copy(tab3[:, :, 0, :], tab_sb[:]).then_inc(tab_step, 1)
            act.wait_ge(s_small_ids[1], 16)
            cast_ids(0, 1)
            cast_ids(0, 2)
            act.wait_ge(s_cst, 16)
            copy_a1t(0)
            act.wait_ge(s_small_ids[2], 16)
            cast_ids(0, 3)
            act.wait_ge(tab_step, 2)
            nc.scalar.copy(tab3[:, :, 1, :], tab_r[:]).then_inc(tab_step, 1)
            copy_a1t(1)
            copy_coefficients(0)
            for n in range(4, NS):
                cast_ids(0, n)
            for g in range(2, G):
                copy_a1t(g)
                copy_coefficients(g - 1)
            copy_coefficients(G - 1)
            act.wait_ge(s_small_ids[3], 16)
            for n in range(NS):
                cast_ids(1, n)
            act.wait_ge(e_pad, 1)
            act.wait_ge(oh_taken, NS)
            windows_a(0, 0, 0)
            chunk(0, 0, 0, first=True)
            chunk(1, 1, 0)
            chunk(2, 0, 1)
            with act.Fori(0, 2) as i:
                chunk(2 * i + 3, 1, i + 1, late_rows=True)
                chunk(2 * i + 4, 0, i + 2)
            chunk(T - 1, 1, T // 2 - 1, last=True)
            relu1(T - 1)
            relu2(T - 1)
            copy_y(T - 1)


def kernel(**inputs):
    import numpy as np
    import ml_dtypes
    import concourse.bacc as bacc
    from concourse.bass_utils import run_bass_kernel_spmd as run

    nc = bacc.Bacc("TRN2", target_bir_lowering=False, num_devices=1)
    arrays = {}

    def give(name, a):
        a = np.ascontiguousarray(a)
        arrays["in_" + name] = a
        return nc.dram_tensor("in_" + name, a.shape, mybir.dt.from_np(a.dtype), kind="ExternalInput").ap()

    dense = np.asarray(inputs["dense_ctx"])
    w_top1 = np.asarray(inputs["W_top1"])
    ids = give("ids", inputs["ids"])
    tables = [give(f"tbl_{f}", inputs[f"tbl_{f}"]) for f in range(S)]
    x0_rows = np.zeros((B, G * GF, H), np.float32)
    x0_rows[:, 0:F] = np.asarray(inputs["r_x0"])
    x0 = give("r_x0", x0_rows.reshape(P, T, G, GF, HP, 2).transpose(1, 2, 5, 3, 4, 0).reshape(T, G, HI, HP * P))
    w_top1_z = give("w_top1_z", w_top1[0:K * H].reshape(K, H, N1).transpose(1, 0, 2).reshape(K * H, N1))
    w_top1_d = give("w_top1_d", w_top1[K * H:])
    w_top2 = give("w_top2", inputs["W_top2"])
    dense_t = give("dense_t", dense.reshape(P, T, DC).transpose(2, 1, 0).reshape(DC, B))
    alpha_rows = np.zeros((G * P, K), np.float32)
    alpha_rows[0:S * F] = np.asarray(inputs["L0_rec_alpha"])
    params = give("params", np.concatenate(
        [alpha_rows.reshape(G, P, K).transpose(1, 0, 2).reshape(P, G * K),
         np.asarray(inputs["L0_rec_w"]).transpose(2, 0, 1).reshape(2, P, H).transpose(1, 0, 2).reshape(P, 2 * H),
         np.asarray(inputs["L0_rec_hv"])[:, :, 0].T.reshape(2, P).T,
         np.asarray(inputs["b_top1"]).reshape(M1, P).T,
         np.asarray(inputs["b_top2"]).reshape(M2, P).T,
         np.asarray(inputs["W_top3"]).reshape(M2, P).T], axis=1))

    small = small_tables([inputs[f"tbl_{f}"].shape[0] for f in range(S)])
    tab_small = give("tab_small", np.concatenate([np.asarray(inputs[f"tbl_{f}"]).reshape(LP, j, D) for f, j in small],
                                                 axis=1))
    ids_small = np.asarray(inputs["ids"])[:, [f for f, j in small]]
    small_ids = give("small_ids", ids_small.reshape(P, 2, T2, len(small)).transpose(1, 3, 2, 0)
                     .reshape(1, 2, len(small), HB))

    starts = np.array([q0 + 13 * (m // 2) + step * (m % 2) for q0, step in GRID for m in range(GF)])
    n = np.arange(P)[:, None, None, None, None]
    g = np.arange(G)[None, :, None, None, None]
    d = np.arange(D)[None, None, :, None, None]
    i = np.arange(GF)[None, None, None, None, :]
    r = np.arange(R)[None, None, None, :, None]
    field = g * GF + i
    flat = D * (g * P + n) + d
    meet = (n // S == i) & (field < F) & (flat // F == starts[field] + r)
    meets = give("meets", meet.reshape(P, G, D, W).astype(ml_dtypes.bfloat16))
    p = np.arange(P)[:, None]
    of_h = p % HI // GF == np.arange(2)[None, :]
    rows = [p * j + np.arange(j)[None, :] for f, j in small]
    consts = give("consts", np.concatenate(
        [np.eye(P), p % K == np.arange(K)[None, :], of_h] + rows, axis=1).astype(np.float32))
    out = nc.dram_tensor("out_y", (B, 1), F32, kind="ExternalOutput").ap()

    tower(nc, ids, small_ids, tables, tab_small, x0, w_top1_z, w_top1_d, w_top2, dense_t, params, meets, consts,
          small, out)
    result = run(nc, [arrays], core_ids=[0])
    return result.results[0]["out_y"]
```

```python
from contextlib import ExitStack

import concourse.bass as bass
from concourse import mybir

F32 = mybir.dt.float32
BF16 = mybir.dt.bfloat16
F16 = mybir.dt.float16
I32 = mybir.dt.int32
ALU = mybir.AluOpType
ACT = mybir.ActivationFunctionType
AX = mybir.AxisListType

P = 128
B = 1024
T = B // P
S = 16
D = 16
Q = S * D
F = 39
K = 16
H = D
R = 8
GF = P // (2 * R)
G = -(-F // GF)
W = GF * R
HI = 2 * GF
HP = H // 2
N1, N2 = 512, 256
M1 = N1 // P
DC = 16
EPAD = Q + 2 * R
GA = 3
FIELDS_A = 10
LP = 125
LMAX = 10
T2 = T // 2
HB = T2 * P


def window_grid():
    width = S * K
    grid = []
    for g in range(G):
        fields = range(g * GF, min((g + 1) * GF, F))
        bounds = [(max(0, (width * i + width - 1) // F - R + 1), width * i // F) for i in fields]
        fits = [(q0, step) for q0 in range(bounds[0][0], bounds[0][1] + 1) for step in (6, 7)
                if all(lo <= q0 + 13 * (n // 2) + step * (n % 2) <= hi for n, (lo, hi) in enumerate(bounds))]
        grid.append(fits[0])
    return grid


GRID = window_grid()
assert GRID[GA][0] >= FIELDS_A * D - R and GRID[GA - 1][0] + 13 * 3 + 7 + R <= FIELDS_A * D


def small_tables(rows):
    return [(f, n // LP) for f, n in enumerate(rows) if n % LP == 0 and n <= LP * LMAX]


def tower(nc, ids, small_ids, tables, tab_small, x0, w_top1_z, w_top1_d, w_top2, b_top2, w_top3, dense_t,
          params, meets, pick, identity, small, out):
    NS = len(small)
    AT = [sum(j for f, j in small[:n]) for n in range(NS + 1)]
    SLOTS = AT[NS]
    large = [f for f in range(S) if f not in [f for f, j in small]]
    large_a = [f for f in large if f < FIELDS_A]
    large_b = [f for f in large if f >= FIELDS_A]
    NA = len([f for f, j in small if f < FIELDS_A])
    assert (NS, NA, G) == (6, 3, 5)
    late = [[], list(range(NA, NA + 1)), list(range(NA + 1, NS))]

    oh_at = [2 * AT[n] for n in range(NA + 1)]
    for n in range(NA + 1, NS):
        oh_at.append(AT[n] - AT[NA + 1])
    assert AT[NS] - AT[NA + 1] <= 2 * AT[1]
    OH_SLOTS = 2 * AT[NA] + small[NA][1]
    ACT_EARLY, ACT_LATE = 2, (3, 2)

    def act_slots(late_part):
        return range(AT[NS] - (sum(ACT_LATE) if late_part else ACT_EARLY), AT[NS])

    with ExitStack() as ctx:
        def sb(name, shape, dt=F32):
            return ctx.enter_context(nc.sbuf_tensor(name, shape, dt))

        def psum(name, shape, dt=F32):
            return ctx.enter_context(nc.psum_tensor(name, shape, dt))

        def sem(name):
            return ctx.enter_context(nc.semaphore(name))

        ids_sb = sb("ids_sb", [P, T, S], I32)
        ident = sb("ident", [P, P])
        meets_sb = sb("meets_sb", [P, G, D, W], BF16)
        params_sb = sb("params_sb", [P, G * K + 2 * H + 2 + M1 + K + 2 + SLOTS + 1])
        alpha_sb = params_sb[:, 0:G * K].rearrange("p (g k) -> p g k", k=K)
        w_sb = params_sb[:, G * K:G * K + 2 * H].rearrange("p (q h) -> p q h", h=H)
        hv_sb = params_sb[:, G * K + 2 * H:G * K + 2 * H + 2]
        b1_sb = params_sb[:, G * K + 2 * H + 2:][:, 0:M1]
        same_k = params_sb[:, G * K + 2 * H + 2 + M1:][:, 0:K]
        of_h = params_sb[:, G * K + 2 * H + 2 + M1 + K:][:, 0:2]
        one = params_sb[:, G * K + 2 * H + 2 + M1 + K + 2 + SLOTS:]
        slot_row = params_sb[:, G * K + 2 * H + 2 + M1 + K + 2:][:, 0:SLOTS]
        alpha_pad = sb("alpha_pad", [P, G, 3, 2 * P - K], BF16)
        alpha3 = alpha_pad[:, :, :, P - K:P]
        alpha_r = sb("alpha_r", [P, G, K])
        zeros = sb("zeros", [P, 4 * P], BF16)
        wbd = sb("wbd", [P, 2, H, K])
        a1t_sb = sb("a1t_sb", [P, 2, 2, P])
        coef = sb("coef", [P, G, HP, 2, K])
        w1_sb = sb("w1_sb", [P, 2, N1])
        w1d_sb = sb("w1d_sb", [DC, N1])
        w2_sb = sb("w2_sb", [P, M1, N2])
        dense_sb = sb("dense_sb", [DC, B])
        tab3 = sb("tab3", [LP, SLOTS, 3, D], BF16)
        ids_rows16 = sb("ids_rows16", [P, B], F16)
        pick_sb = sb("pick_sb", [P, NS], F16)
        ids_bc = sb("ids_bc", [LP, NS, B], F16)
        distance = sb("distance", [LP, HB], F16)
        onehot = sb("onehot", [LP, OH_SLOTS, HB], BF16)
        x_rep = sb("x_rep", [P, 2, G, HP, P])
        ids_rows = x_rep[0:NS, 1, 2].rearrange("p c b -> p (c b)")[:, 0:B].bitcast(I32)
        tab_sb, tab_r = [x_rep[0:LP, 1, g].rearrange("p c b -> p (c b)")[:, 0:SLOTS * D]
                         .rearrange("p (j d) -> p j d", d=D) for g in range(2)]
        e_sb = sb("e_sb", [P, T, EPAD])
        e_both = sb("e_both", [P, 2, G, R, 2, GF])
        x_sb = sb("x_sb", [P, G, HP, P])
        z_sb = sb("z_sb", [P, 2, 2, P])
        h1_sb = sb("h1_sb", [P, M1, P])
        h2_sb = sb("h2_sb", [P, N2])
        h2w_sb = sb("h2w_sb", [P, N2])
        b2_sb = sb("b2_sb", [P, N2])
        w3_sb = sb("w3_sb", [P, N2])
        y_sb = sb("y_sb", [P, T])
        ea = [psum(f"ea{i}", [P, 4, P]) for i in range(2)]
        eb = [psum(f"eb{i}", [P, 4, P]) for i in range(2)]
        hp1 = [psum(f"hp1_{i}", [P, 4, P]) for i in range(2)]
        zp = psum("zp", [P, 4, P])
        hp2 = psum("hp2", [P, 4, P])

        s_ids = sem("s_ids")
        s_ident = sem("s_ident")
        s_params = sem("s_params")
        s_meets = [sem(f"s_meets_{i}") for i in range(3)]
        s_small_ids = sem("s_small_ids")
        rows_zero = sem("rows_zero")
        rows_cast = sem("rows_cast")
        bc_done = sem("bc_done")
        ids_cast = sem("ids_cast")
        s_tab = sem("s_tab")
        s_w1 = sem("s_w1")
        s_w2 = sem("s_w2")
        s_w3 = sem("s_w3")
        s_xa = [sem("s_xa_0"), sem("s_xa_1")]
        s_xb = [sem("s_xb_0"), sem("s_xb_1")]
        s_ea = [sem("s_ea_0"), sem("s_ea_1")]
        s_eb = [sem("s_eb_0"), sem("s_eb_1")]
        e_pad = sem("e_pad")
        tab_step = sem("tab_step")
        tab_ready = sem("tab_ready")
        oh_ready = sem("oh_ready")
        oh_done = sem("oh_done")
        oh_taken = sem("oh_taken")
        abs_ready = sem("abs_ready")
        act_oh_ready = sem("act_oh_ready")
        split_step = sem("split_step")
        alpha_split = sem("alpha_split")
        wbd_ready = sem("wbd_ready")
        zeros_ready = sem("zeros_ready")
        pad_ready = sem("pad_ready")
        a1t_done = sem("a1t_done")
        a1t_copied = sem("a1t_copied")
        coef_done = sem("coef_done")
        coef_ready = sem("coef_ready")
        wina_ready = sem("wina_ready")
        winb_ready = sem("winb_ready")
        eta_done = sem("eta_done")
        etb_done = sem("etb_done")
        x_ready = sem("x_ready")
        z_done = sem("z_done")
        z_ready = sem("z_ready")
        h1_done = sem("h1_done")
        h1_ready = sem("h1_ready")
        h2_done = sem("h2_done")
        h2_ready = sem("h2_ready")
        y_ready = sem("y_ready")
        s_out = sem("s_out")

        def flat(bank):
            return bank.rearrange("p a b -> p (a b)")

        def a1t_bank(g):
            return [zp, hp2][g % 2][:, 0:2, 0:W]

        def coef_bank(g):
            return flat([ea[0], ea[1], ea[0], ea[1], hp1[1]][g][:, 0:2, :])

        def bc_bank(n, half):
            return [ea, eb, hp1][min(n, 2)][half]

        def batch_part(n, late_part):
            return slice(0, T) if n < NA else slice(T2, T) if late_part else slice(0, T2)

        def oh_of(n, late_part, j):
            if n < NA:
                at = oh_at[n] + 2 * (j - AT[n])
                return onehot[:, at:at + 2, :].rearrange("p a b -> p (a b)")
            return onehot[:, oh_at[n] + j - AT[n], :]

        def oh_bank(n, late_part):
            chunks = batch_part(n, late_part)
            bank = hp1[n % 2] if late_part else eb[n % 2]
            return flat(bank[:])[:, 0:(chunks.stop - chunks.start) * 3 * D].rearrange("p (t s d) -> p t s d", s=3, d=D)

        def lookup_at(n, late_part):
            return NS + n - NA if late_part else n

        block = ctx.enter_context(nc.Block())

        @block.sync
        def _(sp):
            def load_meets(n, gs):
                sp.dma_start(meets_sb[:, gs], meets[:, gs]).then_inc(s_meets[n], 16)

            sp.dma_start(ids_sb[:], ids.rearrange("(p t) f -> p t f", t=T)).then_inc(s_ids, 16)
            sp.dma_start(ids_rows, small_ids).then_inc(s_small_ids, 16)
            sp.dma_start(pick_sb[:], pick).then_inc(s_small_ids, 16)
            sp.dma_start(params_sb[:], params).then_inc(s_params, 16)
            load_meets(0, slice(0, 1))
            sp.dma_start(tab_sb, tab_small).then_inc(s_tab, 16)
            load_meets(1, slice(1, 3))
            load_meets(2, slice(3, G))
            sp.dma_start(ident[:], identity).then_inc(s_ident, 16)

            def load_x0(t, slot, gs, landed):
                src = x0[bass.ds(t, 1), gs.start:gs.stop].rearrange("t g q n -> q (t g) n")
                for place in range(R):
                    sp.dma_start(x_rep[HI * place:HI * (place + 1), slot, gs.start:gs.stop, :, :]
                                 .rearrange("q g c b -> q g (c b)"), src).then_inc(landed, 16)

            load_x0(0, 0, range(GA), s_xa[0])
            load_x0(0, 0, range(GA, G), s_xb[0])
            sp.dma_start(w1_sb[:], w_top1_z.rearrange("(q p) n -> p q n", p=P)).then_inc(s_w1, 16)
            sp.dma_start(w1d_sb[:], w_top1_d).then_inc(s_w1, 16)
            sp.dma_start(dense_sb[:], dense_t).then_inc(s_w1, 16)
            sp.dma_start(w2_sb[:], w_top2.rearrange("(m p) n -> p m n", p=P)).then_inc(s_w2, 16)
            sp.dma_start(b2_sb[:], b_top2.broadcast_to([P, N2])).then_inc(s_w3, 16)
            sp.dma_start(w3_sb[:], w_top3.broadcast_to([P, N2])).then_inc(s_w3, 16)
            sp.wait_ge(tab_ready, 1)
            load_x0(1, 1, range(GA), s_xa[1])
            load_x0(1, 1, range(GA, G), s_xb[1])
            with sp.Fori(1, T // 2) as i:
                for slot in range(2):
                    sp.wait_ge(x_ready, (2 * i + slot - 2) * G + GA)
                    load_x0(2 * i + slot, slot, range(GA), s_xa[slot])
                    sp.wait_ge(x_ready, (2 * i + slot - 1) * G)
                    load_x0(2 * i + slot, slot, range(GA, G), s_xb[slot])
            sp.wait_ge(y_ready, T)
            sp.dma_start(out.rearrange("(p t) o -> p (t o)", t=T), y_sb[:]).then_inc(s_out, 16)
            sp.wait_ge(s_out, 16)

        @block.gpsimd
        def _(pool):
            nc.gpsimd.memset(e_sb[:, :, Q:], 0.0).then_inc(e_pad, 1)
            pool.wait_ge(s_ids, 16)
            for t in range(T):
                for s_e, fields in ((s_ea, large_a), (s_eb, large_b)):
                    if t >= 2:
                        pool.wait_ge(s_e[t % 2], 16 * len(fields) * (t // 2))
                    for f in fields:
                        pool.indirect_dma_start(e_sb[:, t, f * D:(f + 1) * D], None, tables[f],
                                                bass.IndirectOffsetOnAxis(ids_sb[:, t, f:f + 1], 0))\
                            .then_inc(s_e[t % 2], 16)

        @block.tensor
        def _(pe):
            def keep_warm(n):
                for _ in range(n):
                    nc.tensor.matmul(flat(hp1[0][:]), zeros[:, 0:P], zeros[:], start=True, stop=True)

            def spread_ids(n):
                if n >= 3:
                    pe.wait_ge(ids_cast, n)
                for half in range(2):
                    last = nc.tensor.matmul(flat(bc_bank(n, half)[0:LP]), pick_sb[:, n:n + 1].broadcast_to([P, LP]),
                                            ids_rows16[:, half * HB:(half + 1) * HB], start=True, stop=True)
                last.then_inc(bc_done, 1)

            def look_up(n, late_part):
                pe.wait_ge(oh_ready, lookup_at(n, late_part) + 1)
                if n == NS - 1:
                    pe.wait_ge(act_oh_ready, ACT_EARLY + late_part * sum(ACT_LATE))
                if not late_part and n >= 2:
                    pe.wait_ge(oh_taken, n - 1)
                chunks = batch_part(n, late_part)
                for c in range(chunks.stop - chunks.start):
                    for j in range(AT[n], AT[n + 1]):
                        last = nc.tensor.matmul(oh_bank(n, late_part)[:, c, :, :],
                                                oh_of(n, late_part, j)[:, c * P:(c + 1) * P],
                                                tab3[:, j, :, :], start=(j == AT[n]), stop=(j == AT[n + 1] - 1))
                last.then_inc(oh_done, 1)

            def a1t(g):
                if g in (0, 1, 3):
                    pe.wait_ge(s_meets[(g + 1) // 2], 16)
                if g >= 2:
                    pe.wait_ge(a1t_copied, g - 1)
                for dh in range(2):
                    for d in range(D // 2):
                        for part in range(3):
                            first = dh == 0 and d == 0 and part == 0
                            last = nc.tensor.matmul(
                                a1t_bank(g)[:, dh, :], alpha_pad[:, g, part, P - K - K * d:2 * P - K - K * d],
                                meets_sb[:, g, dh * D // 2 + d, :], start=first,
                                stop=(d == D // 2 - 1 and part == 2), skip_group_check=True)
                last.then_inc(a1t_done, 1)

            def coefficients(g):
                pe.wait_ge(a1t_copied, g + 1)
                if g == 0:
                    pe.wait_ge(ids_cast, 1)
                if g in (2, 3):
                    pe.wait_ge(coef_ready, g - 1)
                if g == 4:
                    pe.wait_ge(ids_cast, NS)
                for dh in range(2):
                    last = nc.tensor.matmul(coef_bank(g), a1t_sb[:, g % 2, dh, :], wbd[:, dh, :, :],
                                            start=(dh == 0), stop=(dh == 1))
                last.then_inc(coef_done, 1)

            pe.wait_ge(zeros_ready, 1)
            keep_warm(7)
            pe.wait_ge(rows_cast, 1)
            pe.wait_ge(s_small_ids, 32)
            for n in range(3):
                spread_ids(n)
            pe.wait_ge(alpha_split, 1)
            a1t(0)
            a1t(1)
            pe.wait_ge(wbd_ready, 1)
            coefficients(0)
            a1t(2)
            spread_ids(3)
            pe.wait_ge(tab_ready, 1)
            look_up(0, False)
            coefficients(1)
            spread_ids(4)
            coefficients(2)
            look_up(1, False)
            spread_ids(5)
            a1t(3)
            look_up(2, False)
            a1t(4)
            look_up(3, False)

            def windows_a(t, slot):
                pe.wait_ge(wina_ready, t + 1)
                for g in range(GA):
                    last = nc.tensor.transpose(ea[slot][:, g, :],
                                               e_both[:, slot, g].rearrange("p r h i -> p (r h i)"), ident[:])
                last.then_inc(eta_done, 1)

            def windows_b(t, slot):
                pe.wait_ge(winb_ready, t + 1)
                for g in range(GA, G):
                    last = nc.tensor.transpose(eb[slot][:, g - GA, :],
                                               e_both[:, slot, g].rearrange("p r h i -> p (r h i)"), ident[:])
                last.then_inc(etb_done, 1)

            def z_sum(t, slot, g):
                pe.wait_ge(x_ready, t * G + g + 1)
                for pair in range(HP):
                    zh, c = pair // 4, pair % 4
                    last = nc.tensor.matmul(zp[32 * c:32 * c + 32, zh, :],
                                            coef[:, g, pair, :, :].rearrange("p h k -> p (h k)"),
                                            x_sb[:, g, pair, :],
                                            start=(g == 0 and zh == 0), stop=(g == G - 1), skip_group_check=True)
                last.then_inc(z_done, 1)

            def layer1(t, slot):
                for m in range(M1):
                    nc.tensor.matmul(hp1[m // 2][:, m % 2, :], w1d_sb[:, m * P:(m + 1) * P],
                                     dense_sb[:, bass.ds(t * P, P)], start=(m % 2 == 0), stop=False,
                                     skip_group_check=True)
                pe.wait_ge(z_ready, t + 1)
                for half in range(2):
                    for m in range(M1 // 2):
                        cols = slice((2 * half + m) * P, (2 * half + m + 1) * P)
                        for k in range(2):
                            last = nc.tensor.matmul(hp1[half][:, m, :], w1_sb[:, k, cols], z_sb[:, slot, k, :],
                                                    start=False, stop=(k == 1), skip_group_check=True)
                    last.then_inc(h1_done, 1)

            def layer2(t):
                if not (isinstance(t, int) and t == 0):
                    pe.wait_ge(h2_ready, t)
                for k in range(M1):
                    pe.wait_ge(h1_ready, M1 * t + k + 1)
                    last = nc.tensor.matmul(flat(hp2[:])[:, 0:N2], h1_sb[:, k, :], w2_sb[:, k, :],
                                            start=(k == 0), stop=(k == M1 - 1))
                last.then_inc(h2_done, 1)

            def chunk(t, slot, first=False, last=False):
                if not first:
                    if isinstance(t, int) and t < len(late):
                        pe.wait_ge(oh_taken, NS + sum(len(n) for n in late[:t]))
                    layer1(t - 1, 1 - slot)
                if first:
                    look_up(4, False)
                    coefficients(3)
                    look_up(5, False)
                    coefficients(4)
                    pe.wait_ge(coef_ready, G)
                    z_sum(t, slot, 0)
                    pe.wait_ge(oh_taken, NS)
                    windows_b(t, slot)
                else:
                    windows_b(t, slot)
                    z_sum(t, slot, 0)
                z_sum(t, slot, 1)
                if not first:
                    layer2(t - 1)
                z_sum(t, slot, 2)
                if not last:
                    windows_a(t + 1, 1 - slot)
                if isinstance(t, int) and t < len(late):
                    for n in late[t]:
                        look_up(n, True)
                z_sum(t, slot, 3)
                z_sum(t, slot, 4)

            pe.wait_ge(s_ident, 16)
            pe.wait_ge(coef_ready, 3)
            windows_a(0, 0)
            chunk(0, 0, first=True)
            pe.wait_ge(s_w1, 48)
            pe.wait_ge(s_w2, 16)
            chunk(1, 1)
            chunk(2, 0)
            pe.wait_ge(oh_taken, 2 * NS - NA)
            with pe.Fori(0, 2) as i:
                chunk(2 * i + 3, 1)
                chunk(2 * i + 4, 0)
            chunk(T - 1, 1, last=True)
            layer1(T - 1, 1)
            layer2(T - 1)

        @block.vector
        def _(dve):
            steps = [0]

            def step(ins):
                steps[0] += 1
                ins.then_inc(split_step, 1)
                dve.wait_ge(split_step, steps[0])

            def make_onehots(n, late_part, js=None):
                dve.wait_ge(ids_cast, n + 1)
                if late_part:
                    dve.wait_ge(oh_done, n + 1)
                elif n > NA:
                    dve.wait_ge(oh_done, 1)
                batch = slice(batch_part(n, late_part).start * P, batch_part(n, late_part).stop * P)
                end = act_slots(late_part).start if n == NS - 1 else AT[n + 1]
                for j in js or range(AT[n], end):
                    last = nc.vector.tensor_scalar(oh_of(n, late_part, j), ids_bc[:, n, batch],
                                                   slot_row[0:LP, j:j + 1], None, ALU.is_equal)
                    if j == end - 1:
                        last.then_inc(oh_ready, 1)

            def take_rows(n, late_part):
                dve.wait_ge(oh_done, lookup_at(n, late_part) + 1)
                f = small[n][0]
                nc.vector.tensor_reduce(e_sb[:, batch_part(n, late_part), f * D:(f + 1) * D],
                                        oh_bank(n, late_part).rearrange("p t s d -> p t d s"),
                                        AX.X, ALU.add).then_inc(oh_taken, 1)

            nc.vector.memset(zeros[:], 0.0).then_inc(zeros_ready, 1)
            nc.vector.memset(ids_rows16[:], 0.0).then_inc(rows_zero, 1)
            nc.vector.memset(alpha_pad[:], 0.0).then_inc(pad_ready, 1)
            dve.wait_ge(s_small_ids, 32)
            dve.wait_ge(rows_zero, 1)
            nc.vector.tensor_copy(ids_rows16[0:NS], ids_rows).then_inc(rows_cast, 1)
            dve.wait_ge(pad_ready, 1)
            dve.wait_ge(s_params, 16)
            step(nc.vector.tensor_copy(alpha3[:, :, 0, :], alpha_sb))
            step(nc.vector.tensor_tensor(alpha_r[:], alpha_sb, alpha3[:, :, 0, :], ALU.subtract))
            step(nc.vector.tensor_copy(alpha3[:, :, 1, :], alpha_r[:]))
            nc.vector.tensor_tensor(alpha3[:, :, 2, :], alpha_r[:], alpha3[:, :, 1, :], ALU.subtract)\
              .then_inc(alpha_split, 1)
            for dh in range(2):
                last = nc.vector.scalar_tensor_tensor(
                    out=wbd[:, dh, :, :], in0=w_sb[:, dh, :].unsqueeze(2).broadcast_to([P, H, K]),
                    scalar=hv_sb[:, dh:dh + 1], in1=same_k.unsqueeze(1).broadcast_to([P, H, K]),
                    op0=ALU.mult, op1=ALU.mult)
            last.then_inc(wbd_ready, 1)
            make_onehots(0, False, range(AT[0], AT[1] // 2))
            dve.wait_ge(tab_step, 1)
            nc.vector.tensor_tensor(tab_r, tab_sb, tab3[:, :, 0, :], ALU.subtract).then_inc(tab_step, 1)
            make_onehots(0, False, range(AT[1] // 2, AT[1]))
            dve.wait_ge(tab_step, 3)
            nc.vector.tensor_tensor(tab3[:, :, 2, :], tab_r, tab3[:, :, 1, :], ALU.subtract).then_inc(tab_ready, 1)
            make_onehots(1, False)
            make_onehots(2, False)
            take_rows(0, False)
            take_rows(1, False)
            make_onehots(3, False)
            take_rows(2, False)
            make_onehots(4, False)
            make_onehots(5, False)
            take_rows(3, False)
            take_rows(4, False)

            def products(t, slot, uses, g):
                if g == 0:
                    dve.wait_ge(s_xa[slot], 16 * R * (uses + 1))
                    dve.wait_ge(eta_done, t + 1)
                if g == GA:
                    dve.wait_ge(s_xb[slot], 16 * R * (uses + 1))
                    dve.wait_ge(etb_done, t + 1)
                if not (isinstance(t, int) and t == 0):
                    dve.wait_ge(z_done, (t - 1) * G + g + 1)
                window = ea[slot][:, g, :] if g < GA else eb[slot][:, g - GA, :]
                nc.vector.tensor_tensor(x_sb[:, g, :, :], x_rep[:, slot, g, :, :],
                                        window.unsqueeze(1).broadcast_to([P, HP, P]), ALU.mult).then_inc(x_ready, 1)

            NL = 2 * G - 1
            slots = [(n, j) for n in range(NA, NS) for j in range(AT[n], AT[n + 1])
                     if j not in act_slots(True)]
            late_slots = [slots[len(slots) * max(0, i - G) // NL:len(slots) * max(0, min(i + 1 - G, NL)) // NL]
                          for i in range(3 * G)]

            def output(t):
                dve.wait_ge(h2_done, t + 1)
                if not (isinstance(t, int) and t == 0):
                    dve.wait_ge(y_ready, t)
                nc.vector.tensor_tensor(h2_sb[:], flat(hp2[:])[:, 0:N2], b2_sb[:], ALU.add).then_inc(h2_ready, 1)
                dve.wait_ge(h2_ready, t + 1)
                nc.vector.scalar_tensor_tensor(out=h2w_sb[:], in0=h2_sb[:], scalar=0.0, in1=w3_sb[:], op0=ALU.max,
                                               op1=ALU.mult, accum_out=y_sb[:, bass.ds(t, 1)]).then_inc(y_ready, 1)

            for t in range(3):
                for g in range(G):
                    products(t, t % 2, t // 2, g)
                    if t == 0 and g == 0:
                        take_rows(5, False)
                    if g == G - 1:
                        for n in late[t]:
                            take_rows(n, True)
                    for n, j in late_slots[G * t + g]:
                        make_onehots(n, True, [j])
                if t == 1:
                    dve.wait_ge(s_w3, 32)
                if t >= 1:
                    output(t - 1)
            with dve.Fori(0, 2) as i:
                for g in range(G):
                    products(2 * i + 3, 1, i + 1, g)
                output(2 * i + 2)
                for g in range(G):
                    products(2 * i + 4, 0, i + 2, g)
                output(2 * i + 3)
            for g in range(G):
                products(T - 1, 1, T // 2 - 1, g)
            output(T - 2)
            output(T - 1)

        @block.scalar
        def _(act):
            def cast_ids(n):
                act.wait_ge(bc_done, n + 1)
                for half in range(2):
                    last = nc.scalar.copy(ids_bc[:, n, half * HB:(half + 1) * HB], flat(bc_bank(n, half)[0:LP]))
                last.then_inc(ids_cast, 1)

            made = [0]

            def make_onehots(late_part, js):
                n = NS - 1
                act.wait_ge(ids_cast, NS)
                act.wait_ge(oh_done, n + 1 if late_part else 1)
                chunks = batch_part(n, late_part)
                for j in js:
                    if made[0]:
                        act.wait_ge(act_oh_ready, made[0])
                    nc.scalar.activation(distance[:], ids_bc[:, n, chunks.start * P:chunks.stop * P], ACT.Abs,
                                         bias=slot_row[0:LP, j:j + 1], scale=-1.0).then_inc(abs_ready, 1)
                    made[0] += 1
                    act.wait_ge(abs_ready, made[0])
                    nc.scalar.activation(oh_of(n, late_part, j), distance[:], ACT.Relu, bias=one[0:LP],
                                         scale=-1.0).then_inc(act_oh_ready, 1)

            def copy_a1t(g):
                act.wait_ge(a1t_done, g + 1)
                if g >= 2:
                    act.wait_ge(coef_done, g - 1)
                for dh in range(2):
                    last = nc.scalar.copy(
                        a1t_sb[:, g % 2, dh, :].rearrange("p (r h i) -> p r h i", h=2, i=GF),
                        a1t_bank(g)[:, dh, :].rearrange("p (r i) -> p r i", i=GF).unsqueeze(2).broadcast_to([P, R, 2, GF]))
                last.then_inc(a1t_copied, 1)

            def copy_coefficients(g):
                act.wait_ge(coef_done, g + 1)
                found = coef_bank(g).rearrange("p (c h k) -> p c h k", h=2, k=K)
                for h in range(2):
                    last = nc.scalar.activation(coef[:, g, :, h, :], found[:, :, h, :], ACT.Copy,
                                                scale=of_h[:, h:h + 1])
                last.then_inc(coef_ready, 1)

            def take_windows(t, slot, gs):
                for g in gs:
                    q0, stp = GRID[g]
                    base = e_sb[:, bass.ds(t, 1), q0:q0 + R]
                    src = bass.AP(tensor=base.tensor, offset=base.offset,
                                  ap=[base.ap[0], [1, R], [0, 2], [13, GF // 2], [stp, 2]])
                    last = nc.scalar.copy(e_both[:, slot, g].rearrange("p r h (j m) -> p r h j m", m=2), src)
                return last

            def windows_a(t, slot, uses):
                act.wait_ge(s_ea[slot], 16 * len(large_a) * (uses + 1))
                if not (isinstance(t, int) and t < 2):
                    act.wait_ge(eta_done, t - 1)
                take_windows(t, slot, range(GA)).then_inc(wina_ready, 1)

            def windows_b(t, slot, uses):
                act.wait_ge(s_eb[slot], 16 * len(large_b) * (uses + 1))
                if not (isinstance(t, int) and t < 2):
                    act.wait_ge(etb_done, t - 1)
                take_windows(t, slot, range(GA, G)).then_inc(winb_ready, 1)

            def copy_z(t, slot):
                act.wait_ge(z_done, (t + 1) * G)
                nc.scalar.copy(z_sb[:, slot, :, :], zp[:, 0:2, :]).then_inc(z_ready, 1)

            def relu1(t):
                for m in range(M1):
                    act.wait_ge(h1_done, 2 * t + 1 + m // 2)
                    nc.scalar.activation(h1_sb[:, m, :], hp1[m // 2][:, m % 2, :], ACT.Relu,
                                         bias=b1_sb[:, m:m + 1]).then_inc(h1_ready, 1)

            def chunk(t, slot, uses, first=False, last=False):
                windows_b(t, slot, uses)
                if not first:
                    relu1(t - 1)
                if not last:
                    windows_a(t + 1, 1 - slot, uses + slot)
                if isinstance(t, int) and t == 1:
                    make_onehots(True, act_slots(True)[:ACT_LATE[0]])
                if isinstance(t, int) and t == 2:
                    make_onehots(True, act_slots(True)[ACT_LATE[0]:])
                copy_z(t, slot)

            cast_ids(0)
            act.wait_ge(s_tab, 16)
            nc.scalar.copy(tab3[:, :, 0, :], tab_sb).then_inc(tab_step, 1)
            cast_ids(1)
            act.wait_ge(s_params, 16)
            copy_a1t(0)
            cast_ids(2)
            act.wait_ge(tab_step, 2)
            nc.scalar.copy(tab3[:, :, 1, :], tab_r).then_inc(tab_step, 1)
            copy_a1t(1)
            copy_coefficients(0)
            copy_a1t(2)
            cast_ids(3)
            copy_coefficients(1)
            copy_coefficients(2)
            cast_ids(4)
            cast_ids(5)
            copy_a1t(3)
            make_onehots(False, act_slots(False))
            copy_a1t(4)
            act.wait_ge(e_pad, 1)
            act.wait_ge(oh_taken, NA)
            windows_a(0, 0, 0)
            copy_coefficients(3)
            copy_coefficients(4)
            act.wait_ge(oh_taken, NS)
            chunk(0, 0, 0, first=True)
            chunk(1, 1, 0)
            chunk(2, 0, 1)
            with act.Fori(0, 2) as i:
                chunk(2 * i + 3, 1, i + 1)
                act.wait_ge(oh_taken, 2 * NS - NA)
                chunk(2 * i + 4, 0, i + 2)
            chunk(T - 1, 1, T // 2 - 1, last=True)
            relu1(T - 1)


def kernel(**inputs):
    import numpy as np
    import ml_dtypes
    import concourse.bacc as bacc
    from concourse.bass_utils import run_bass_kernel_spmd as run

    nc = bacc.Bacc("TRN2", target_bir_lowering=False, num_devices=1)
    arrays = {}

    def give(name, a):
        a = np.ascontiguousarray(a)
        arrays["in_" + name] = a
        return nc.dram_tensor("in_" + name, a.shape, mybir.dt.from_np(a.dtype), kind="ExternalInput").ap()

    dense = np.asarray(inputs["dense_ctx"])
    w_top1 = np.asarray(inputs["W_top1"])
    ids = give("ids", inputs["ids"])
    tables = [give(f"tbl_{f}", inputs[f"tbl_{f}"]) for f in range(S)]
    x0_rows = np.zeros((B, G * GF, H), np.float32)
    x0_rows[:, 0:F] = np.asarray(inputs["r_x0"])
    x0 = give("r_x0", x0_rows.reshape(P, T, G, GF, HP, 2).transpose(1, 2, 5, 3, 4, 0).reshape(T, G, HI, HP * P))
    w_top1_z = give("w_top1_z", w_top1[0:K * H].reshape(K, H, N1).transpose(1, 0, 2).reshape(K * H, N1))
    w_top1_d = give("w_top1_d", w_top1[K * H:])
    w_top2 = give("w_top2", inputs["W_top2"])
    b_top2 = give("b_top2", np.asarray(inputs["b_top2"]).reshape(1, N2))
    w_top3 = give("w_top3", np.asarray(inputs["W_top3"]).reshape(1, N2))
    dense_t = give("dense_t", dense.reshape(P, T, DC).transpose(2, 1, 0).reshape(DC, B))
    alpha_rows = np.zeros((G * P, K), np.float32)
    alpha_rows[0:S * F] = np.asarray(inputs["L0_rec_alpha"])
    params = np.concatenate(
        [alpha_rows.reshape(G, P, K).transpose(1, 0, 2).reshape(P, G * K),
         np.asarray(inputs["L0_rec_w"]).transpose(2, 0, 1).reshape(2, P, H).transpose(1, 0, 2).reshape(P, 2 * H),
         np.asarray(inputs["L0_rec_hv"])[:, :, 0].T.reshape(2, P).T,
         np.asarray(inputs["b_top1"]).reshape(M1, P).T], axis=1)

    small = small_tables([inputs[f"tbl_{f}"].shape[0] for f in range(S)])
    tab_small = give("tab_small", np.concatenate([np.asarray(inputs[f"tbl_{f}"]).reshape(LP, j, D) for f, j in small],
                                                 axis=1))
    ids_small = np.asarray(inputs["ids"])[:, [f for f, j in small]]
    small_ids = give("small_ids", ids_small.reshape(P, T, len(small)).transpose(2, 1, 0).reshape(len(small), B))

    starts = np.array([q0 + 13 * (m // 2) + step * (m % 2) for q0, step in GRID for m in range(GF)])
    n = np.arange(P)[:, None, None, None, None]
    g = np.arange(G)[None, :, None, None, None]
    d = np.arange(D)[None, None, :, None, None]
    i = np.arange(GF)[None, None, None, None, :]
    r = np.arange(R)[None, None, None, :, None]
    field = g * GF + i
    flat = D * (g * P + n) + d
    meet = (n // S == i) & (field < F) & (flat // F == starts[field] + r)
    meets = give("meets", meet.reshape(P, G, D, W).astype(ml_dtypes.bfloat16))
    p = np.arange(P)[:, None]
    of_h = p % HI // GF == np.arange(2)[None, :]
    rows = [p * j + np.arange(j)[None, :] for f, j in small]
    same_k = p % K == np.arange(K)[None, :]
    fixed = np.concatenate([same_k, of_h] + rows + [np.ones((P, 1))], axis=1).astype(np.float32)
    params = give("params", np.concatenate([params, fixed], axis=1))
    pick = give("pick", np.eye(P, len(small), dtype=np.float16))
    identity = give("identity", np.eye(P, dtype=np.float32))
    out = nc.dram_tensor("out_y", (B, 1), F32, kind="ExternalOutput").ap()

    tower(nc, ids, small_ids, tables, tab_small, x0, w_top1_z, w_top1_d, w_top2, b_top2, w_top3, dense_t,
          params, meets, pick, identity, small, out)
    result = run(nc, [arrays], core_ids=[0])
    return result.results[0]["out_y"]
```
